# Optimizing a Trainium2 kernel written in Bass

```python
import numpy as np
import jax
import jax.numpy as jnp

def _softmax(x, axis=-1):
    return jax.nn.softmax(x, axis=axis)

def _gelu(x):
    return jax.nn.gelu(x, approximate=True)

def _silu(x):
    return jax.nn.silu(x)

def _sigmoid(x):
    return jax.nn.sigmoid(x)

def _layernorm(x, axis=-1, eps=1e-05):
    m = jnp.mean(x, axis=axis, keepdims=True)
    v = jnp.var(x, axis=axis, keepdims=True)
    return (x - m) / jnp.sqrt(v + eps)

def _scatter_add(tgt, idx, src, axis=0):
    return tgt.at[idx].add(src)

def _segment_sum(src, seg, n):
    return jax.ops.segment_sum(src, seg, n)
kernel_name = 'mk_gnn_preln_d1_gnn_r64_26ff06'

def setup_inputs(seed: int=0):
    np.random.seed(seed)
    _w = jnp.asarray

    def _rec_inputs():
        import jax
        import jax.numpy as jnp
        _gk = jax.random.key(seed)
        x = -0.0005121 + 1.001 * jax.random.normal(jax.random.fold_in(_gk, 1), (100000, 64), jnp.float32)
        src = jax.random.randint(jax.random.fold_in(_gk, 2), (25000,), 0, 100000, jnp.int32)
        dst = jnp.minimum((100000 * jax.random.uniform(jax.random.fold_in(_gk, 3), (25000,)) ** 2.0).astype(jnp.int32), 99999)
        _o = jnp.argsort(dst, stable=True)
        src = src[_o]
        dst = dst[_o]
        edge_attr_4 = jax.random.uniform(jax.random.fold_in(_gk, 11), (25000, 4), jnp.float32, 0.0, 1)
        return (x, src, dst, edge_attr_4)
    x, src, dst, edge_attr_4 = _rec_inputs()

    def _L0_gnn_setup():
        import jax, jax.numpy as jnp
        import numpy as np
        N, E, C = (50000, 12500, 64)

        def _forward(x, edge_attr, deg_hist, weight, W_e, b_e, W_pre, b_pre, W_post, b_post, W_ih, W_hh, b_ih, b_hh, edge_index):
            n_nodes = x.shape[0]
            avg_log = jnp.mean(jnp.log(deg_hist + 1.0))
            m = x @ weight[0]
            src, dst = (edge_index[0], edge_index[1])
            ew = edge_attr[:, 3:4]
            ea = (edge_attr[:, :3] @ W_e + b_e) * ew
            x_i = m[dst] * ew
            x_j = m[src] * ew
            h = jnp.concatenate([x_i, x_j, ea], axis=-1) @ W_pre + b_pre
            cnt = jax.ops.segment_sum(jnp.ones((h.shape[0],), h.dtype), dst, n_nodes)
            deg = jnp.clip(cnt, 1.0)[:, None]
            mean = jax.ops.segment_sum(h, dst, n_nodes) / deg
            mean_sq = jax.ops.segment_sum(h * h, dst, n_nodes) / deg
            has = (cnt > 0)[:, None]
            mn = jnp.where(has, jax.ops.segment_min(h, dst, n_nodes), 0.0)
            mx = jnp.where(has, jax.ops.segment_max(h, dst, n_nodes), 0.0)
            std = jnp.sqrt(jax.nn.relu(mean_sq - mean * mean) + 1e-05)
            agg = jnp.concatenate([mean, mn, mx, std], axis=-1)
            amp = jnp.log(deg + 1.0) / avg_log
            att = avg_log / jnp.log(deg + 1.0)
            o_id = agg
            o_amp = agg * amp
            o_att = o_amp * att
            out = jnp.concatenate([m, o_id, o_amp, o_att], axis=-1)
            out = out @ W_post + b_post
            gi = out @ W_ih.T + b_ih
            gh = x @ W_hh.T + b_hh
            i_r, i_z, i_n = jnp.split(gi, 3, axis=-1)
            h_r, h_z, h_n = jnp.split(gh, 3, axis=-1)
            r = jax.nn.sigmoid(i_r + h_r)
            z = jax.nn.sigmoid(i_z + h_z)
            n = jnp.tanh(i_n + r * h_n)
            return (1.0 - z) * n + z * x
        key = jax.random.key(seed)
        ks = jax.random.split(key, 16)
        s = 0.1
        return {'x': jax.random.normal(ks[0], (N, C), jnp.float32), 'edge_index': jax.random.randint(ks[1], (2, E), 0, N, dtype=jnp.int32), 'edge_attr': jax.random.uniform(ks[2], (E, 4), jnp.float32), 'deg_hist': jnp.asarray([1.0, 2.0, 4.0, 8.0, 16.0, 32.0, 16.0, 8.0, 4.0, 2.0, 1.0], jnp.float32), 'weight': jax.random.normal(ks[3], (1, C, C), jnp.float32) * s, 'W_e': jax.random.normal(ks[4], (3, C), jnp.float32) * s, 'b_e': jax.random.normal(ks[5], (C,), jnp.float32) * s, 'W_pre': jax.random.normal(ks[6], (3 * C, C), jnp.float32) * s, 'b_pre': jax.random.normal(ks[7], (C,), jnp.float32) * s, 'W_post': jax.random.normal(ks[8], (13 * C, C), jnp.float32) * s, 'b_post': jax.random.normal(ks[9], (C,), jnp.float32) * s, 'W_ih': jax.random.normal(ks[10], (3 * C, C), jnp.float32) * s, 'W_hh': jax.random.normal(ks[11], (3 * C, C), jnp.float32) * s, 'b_ih': jax.random.normal(ks[12], (3 * C,), jnp.float32) * s, 'b_hh': jax.random.normal(ks[13], (3 * C,), jnp.float32) * s}
    _L0_gnn_all = _L0_gnn_setup()
    _L0_gnn_in = {k: v for k, v in _L0_gnn_all.items() if k in ('deg_hist', 'weight', 'W_e', 'b_e', 'W_pre', 'b_pre', 'W_post', 'b_post', 'W_ih', 'W_hh', 'b_ih', 'b_hh')}
    del _L0_gnn_all
    return {'x': x, 'src': src, 'dst': dst, 'edge_attr_4': edge_attr_4, 'L0_gnn_deg_hist': _L0_gnn_in['deg_hist'], 'L0_gnn_weight': _L0_gnn_in['weight'], 'L0_gnn_W_e': _L0_gnn_in['W_e'], 'L0_gnn_b_e': _L0_gnn_in['b_e'], 'L0_gnn_W_pre': _L0_gnn_in['W_pre'], 'L0_gnn_b_pre': _L0_gnn_in['b_pre'], 'L0_gnn_W_post': _L0_gnn_in['W_post'], 'L0_gnn_b_post': _L0_gnn_in['b_post'], 'L0_gnn_W_ih': _L0_gnn_in['W_ih'], 'L0_gnn_W_hh': _L0_gnn_in['W_hh'], 'L0_gnn_b_ih': _L0_gnn_in['b_ih'], 'L0_gnn_b_hh': _L0_gnn_in['b_hh']}

def reference(x, src, dst, edge_attr_4, L0_gnn_deg_hist, L0_gnn_weight, L0_gnn_W_e, L0_gnn_b_e, L0_gnn_W_pre, L0_gnn_b_pre, L0_gnn_W_post, L0_gnn_b_post, L0_gnn_W_ih, L0_gnn_W_hh, L0_gnn_b_ih, L0_gnn_b_hh):
    import jax
    import jax.numpy as jnp

    def _L0_gnn_ref(x, edge_index, edge_attr, deg_hist, weight, W_e, b_e, W_pre, b_pre, W_post, b_post, W_ih, W_hh, b_ih, b_hh):
        import jax, jax.numpy as jnp
        import numpy as np
        N, E, C = (50000, 12500, 64)

        def _forward(x, edge_attr, deg_hist, weight, W_e, b_e, W_pre, b_pre, W_post, b_post, W_ih, W_hh, b_ih, b_hh, edge_index):
            n_nodes = x.shape[0]
            avg_log = jnp.mean(jnp.log(deg_hist + 1.0))
            m = x @ weight[0]
            src, dst = (edge_index[0], edge_index[1])
            ew = edge_attr[:, 3:4]
            ea = (edge_attr[:, :3] @ W_e + b_e) * ew
            x_i = m[dst] * ew
            x_j = m[src] * ew
            h = jnp.concatenate([x_i, x_j, ea], axis=-1) @ W_pre + b_pre
            cnt = jax.ops.segment_sum(jnp.ones((h.shape[0],), h.dtype), dst, n_nodes)
            deg = jnp.clip(cnt, 1.0)[:, None]
            mean = jax.ops.segment_sum(h, dst, n_nodes) / deg
            mean_sq = jax.ops.segment_sum(h * h, dst, n_nodes) / deg
            has = (cnt > 0)[:, None]
            mn = jnp.where(has, jax.ops.segment_min(h, dst, n_nodes), 0.0)
            mx = jnp.where(has, jax.ops.segment_max(h, dst, n_nodes), 0.0)
            std = jnp.sqrt(jax.nn.relu(mean_sq - mean * mean) + 1e-05)
            agg = jnp.concatenate([mean, mn, mx, std], axis=-1)
            amp = jnp.log(deg + 1.0) / avg_log
            att = avg_log / jnp.log(deg + 1.0)
            o_id = agg
            o_amp = agg * amp
            o_att = o_amp * att
            out = jnp.concatenate([m, o_id, o_amp, o_att], axis=-1)
            out = out @ W_post + b_post
            gi = out @ W_ih.T + b_ih
            gh = x @ W_hh.T + b_hh
            i_r, i_z, i_n = jnp.split(gi, 3, axis=-1)
            h_r, h_z, h_n = jnp.split(gh, 3, axis=-1)
            r = jax.nn.sigmoid(i_r + h_r)
            z = jax.nn.sigmoid(i_z + h_z)
            n = jnp.tanh(i_n + r * h_n)
            return (1.0 - z) * n + z * x
        return _forward(x, edge_attr, deg_hist, weight, W_e, b_e, W_pre, b_pre, W_post, b_post, W_ih, W_hh, b_ih, b_hh, edge_index)
    edge_index = jnp.stack([src, dst])
    h = jnp.maximum(_layernorm(x, axis=-1), 0.0)
    x = x + _L0_gnn_ref(h, edge_index, edge_attr_4, L0_gnn_deg_hist, L0_gnn_weight, L0_gnn_W_e, L0_gnn_b_e, L0_gnn_W_pre, L0_gnn_b_pre, L0_gnn_W_post, L0_gnn_b_post, L0_gnn_W_ih, L0_gnn_W_hh, L0_gnn_b_ih, L0_gnn_b_hh)
    return x

_drawn_inputs = setup_inputs


def setup_inputs(seed=0):
    import zlib

    import numpy as np

    out = dict(_drawn_inputs(seed))
    spreads = {}
    factors = {'L0_gnn_deg_hist': 8.0, 'L0_gnn_W_e': 6.139, 'L0_gnn_b_e': 3.516}
    for name, (base, spread) in spreads.items():
        noise = np.random.default_rng([zlib.crc32(name.encode()), seed]).standard_normal(out[name].shape)
        drawn = base * np.exp(spread * noise) if base else spread * noise
        out[name] = jnp.asarray(drawn.astype(out[name].dtype))
    for name, factor in factors.items():
        out[name] = (out[name] * factor).astype(out[name].dtype)
    return out
```

```python
import concourse.bass as bass
from concourse import mybir
from contextlib import ExitStack

NODES, C, EDGES = 100000, 64, 25000
P = 128
BLOCKS = 25
GROUPS = 32
ROWS = P * GROUPS
STRIDE = (NODES - ROWS) // (BLOCKS - 1)
CHUNKS = 4
GC = GROUPS // CHUNKS
TILES = 8
EB = P * TILES
HALF = EB // 2
TH = TILES // 2
ALL_TILES = BLOCKS * TILES
EDGES_PADDED = BLOCKS * EB
RC = EDGES_PADDED // P
OUT_OF_RANGE = 1 << 20
BIG = 1.5e38
EPS = 1e-5
PARTS = 3
AR = 5
KEEP_ROW = PARTS * PARTS * AR
PER_STEP = 31
assert STRIDE * (BLOCKS - 1) + ROWS == NODES and EDGES <= EDGES_PADDED


class At:

    def __init__(self, j, off):
        self.j, self.off = j, off

    def times(self, per, plus=0):
        c = per * self.off + plus
        return c if self.j is None else self.j * (2 * per) + c

    def pair(self, per):
        c = per * (self.off // 2 + 1)
        return c if self.j is None else self.j * per + c

    def next(self, n=1):
        return At(self.j, self.off + n)

    @property
    def par(self):
        return self.off % 2


def wait(e, sem, value):
    if isinstance(value, int) and value <= 0:
        return
    e.wait_ge(sem, value)


def gnn_kernel(nc, x, gidx, key_l, next_l, key_r, prev_r, key_b, attr_r, ew_l, ident, w_t, w_pre, w_post,
               wih_t, whh_t, we_t, b_pre, b_post, bih_c, bhh_c, bih_r, bhh_r, deg_hist, out):
    f32, bf16, i32 = mybir.dt.float32, mybir.dt.bfloat16, mybir.dt.int32
    ALU, ACT, AX = mybir.AluOpType, mybir.ActivationFunctionType, mybir.AxisListType.X

    ctx = ExitStack()
    with ctx:
        def sb(name, shape, dt=f32):
            return ctx.enter_context(nc.sbuf_tensor(name, shape, dt))

        def pb(name, shape):
            return ctx.enter_context(nc.psum_tensor(name, shape, f32))

        def sem(name):
            return ctx.enter_context(nc.semaphore(name))

        cnt_rows = nc.dram_tensor("cnt_rows", (P, RC), f32, kind="Internal").ap()
        keep_rows = nc.dram_tensor("keep_rows", (P, RC), bf16, kind="Internal").ap()
        attr_rows = nc.dram_tensor("attr_rows", (PARTS * AR, P, RC), bf16, kind="Internal").ap()
        wau_rows = nc.dram_tensor("wau_rows", (AR, PARTS, C), bf16, kind="Internal").ap()
        late_cell = nc.dram_tensor("late_cell", (BLOCKS, 1), i32, kind="Internal").ap()
        parked = nc.dram_tensor("parked", (BLOCKS, P, TILES * C), f32, kind="Internal").ap()
        bias_rows = nc.dram_tensor("bias_rows", (1, PARTS, 4 * C), bf16, kind="Internal").ap()

        GIDX = sb("GIDX", [P, ALL_TILES * 2], i32)
        SIDX = sb("SIDX", [P, ALL_TILES], i32)
        COEFS = sb("COEFS", [P, ALL_TILES, 4])
        ID = sb("ID", [P, P])
        DW = sb("DW", [P, 4, P])
        DB = sb("DB", [P, 4])
        QW = sb("QW", [P, P])
        WAUG = sb("WAUG", [P, P], bf16)
        SELK = sb("SELK", [P, P], bf16)
        OW1 = sb("OW1", [P, 3 * C])
        OW2 = sb("OW2", [P, 3 * C])
        SW = sb("SW", [P, 4 * C])
        SBIAS = sb("SBIAS", [P, 2, 4 * C], bf16)
        ONESB = sb("ONESB", [P, P], bf16)
        ATT = [sb(f"ATT{i}", [P, EB], bf16) for i in range(2)]

        X = [sb(f"X{i}", [P, GROUPS, C]) for i in range(2)]
        XN = [sb(f"XN{i}", [P, GROUPS, C]) for i in range(2)]
        SQ = sb("SQ", [P, GROUPS, C])
        HT = [sb(f"HT{i}", [P, 512]) for i in range(2)]
        SR = [sb(f"SR{i}", [P, 512]) for i in range(2)]
        SZ = [sb(f"SZ{i}", [P, 512]) for i in range(2)]
        T = sb("T", [P, 512])
        U = [sb(f"U{i}", [P, 512]) for i in range(2)]
        NN = [sb(f"NN{i}", [P, 512]) for i in range(2)]
        D = sb("D", [P, 512])
        Y = [sb(f"Y{i}", [P, 512]) for i in range(2)]
        SUM = sb("SUM", [P, GROUPS + 2 * TILES])
        MEAN = sb("MEAN", [P, GROUPS + 2 * TILES])
        SSQ = sb("SSQ", [P, GROUPS + 2 * TILES])
        VAR = sb("VAR", [P, GROUPS + 2 * TILES])
        RSTD = sb("RSTD", [P, GROUPS + 2 * TILES])

        IX = [sb(f"IX{i}", [P, 2 * TILES], i32) for i in range(2)]
        XG = [sb(f"XG{i}", [P, TILES, 2, C]) for i in range(2)]
        EC = sb("EC", [P, TILES, 2, C])
        ESQ = sb("ESQ", [P, TILES * 2, C])
        HS = sb("HS", [P, TILES, C])
        V = sb("V", [P, TILES, 2 * C])
        HO = [sb(f"HO{i}", [P, TILES, 2 * C]) for i in range(2)]
        XD = [sb(f"XD{i}", [P, TILES, C]) for i in range(2)]
        COEF = [sb(f"COEF{i}", [P, TILES, 4]) for i in range(2)]
        VTS = sb("VTS", [P, EB])
        H = sb("H", [P, HALF])
        CAP = sb("CAP", [P, HALF])
        S = sb("S", [P, EB])
        MX = [sb(f"MX{i}", [P, EB]) for i in range(2)]
        MS = sb("MS", [P, TILES, 2 * C])
        M2 = sb("M2", [P, TILES, C])
        MST = sb("MST", [P, EB])
        T1 = sb("T1", [P, TH, 2 * C])
        OS = sb("OS", [P, TH, C])
        HOT = sb("HOT", [P, EB])
        RZ = sb("RZ", [P, TILES, 2 * C])
        TG = sb("TG", [P, TH, C])
        UG = sb("UG", [P, TILES, C])
        NG = sb("NG", [P, TILES, C])
        DG = sb("DG", [P, TILES, C])
        RES = [sb(f"RES{i}", [P, TILES, C]) for i in range(2)]
        SIX = [sb(f"SIX{i}", [P, TILES], i32) for i in range(2)]

        TIN = pb("TIN", [P, 512])
        TOUT = pb("TOUT", [P, 512])
        GATE = pb("GATE", [P, 4, 512])
        EP = pb("EP", [P, EB])
        EPT = EP[:, :].rearrange("p (t c) -> p t c", c=2 * C)
        EPW = EP[:, :].rearrange("p (t c) -> p t c", c=4 * C)

        KL = sb("KL", [P, ALL_TILES], i32)
        NL = sb("NL", [P, ALL_TILES], i32)
        KR = sb("KR", [P, RC], i32)
        PR = sb("PR", [P, RC], i32)
        spare = XN[1][:, :, :].rearrange("p g c -> p (g c)")
        AR_IN = spare[:, 0:4 * RC].rearrange("p (k c) -> p k c", k=4)
        EW = sb("EW", [P, ALL_TILES])
        W0 = sb("W0", [P, ALL_TILES])
        W1 = sb("W1", [P, ALL_TILES])
        W2 = sb("W2", [P, ALL_TILES])
        LATE = sb("LATE", [1, BLOCKS + 1], i32)
        LATEC = sb("LATEC", [BLOCKS, 4])
        LATEI = sb("LATEI", [BLOCKS, 1], i32)
        KB = SQ[0:BLOCKS, :, :].rearrange("p g c -> p (g c)")[:, 0:EB].bitcast(i32)
        KBF = SQ[0:BLOCKS, :, :].rearrange("p g c -> p (g c)")[:, EB:2 * EB]
        IDX = sb("IDX", [P, RC])
        KEEP = sb("KEEP", [P, RC], bf16)
        LOC = sb("LOC", [P, RC])
        CARRY = sb("CARRY", [1, P + 1])
        LAST = sb("LAST", [P, 1])
        CNT_R = sb("CNT_R", [P, RC])
        CNT_T = sb("CNT_T", [RC // 2, 2, P])
        AE = spare[:, 4 * RC:(4 + AR) * RC].rearrange("p (k c) -> p k c", k=AR)
        APART = X[1][:, :, :].rearrange("p g c -> p (g c)").bitcast(bf16)[:, 0:PARTS * AR * RC]\
            .rearrange("p (i k c) -> p i k c", i=PARTS, k=AR)
        ONE = sb("ONE", [P, 1])
        ZERO1 = sb("ZERO1", [P, 1])
        WT2 = sb("WT2", [C, 2, C])
        WPRE = sb("WPRE", [C, 3, C])
        WP0 = sb("WP0", [C, C])
        STDW = sb("STDW", [C, 3, C])
        WIHD = sb("WIHD", [C, 3, 2, C])
        WIH2 = sb("WIH2", [P, 3 * C])
        WHH2 = sb("WHH2", [P, 3 * C])
        WET = sb("WET", [C, 4])
        WAU = sb("WAU", [AR, C])
        WAUR = sb("WAUR", [AR, C])
        WAUP = sb("WAUP", [AR, PARTS, C], bf16)
        BPC = sb("BPC", [C, 1])
        BV = sb("BV", [C, 1])
        BIC = sb("BIC", [P, 3])
        BHC = sb("BHC", [P, 3])
        BIR = sb("BIR", [1, 3 * C])
        BHR = sb("BHR", [1, 3 * C])
        BROW = sb("BROW", [1, 4 * C])
        BRES = sb("BRES", [1, 4 * C])
        BPART = sb("BPART", [1, PARTS, 4 * C], bf16)
        DH = sb("DH", [P, 11])
        LDH = sb("LDH", [P, 11])
        AVG = sb("AVG", [P, 1])
        IAVG = sb("IAVG", [P, 1])
        LG = sb("LG", [P, ALL_TILES])
        ILG = sb("ILG", [P, ALL_TILES])
        NOEDGE = sb("NOEDGE", [P, 8])
        M1D = sb("M1D", [C, 2, C])

        names = """setup_loaded ident_loaded zeroed flags_made iota_made logs_ready split_saved split_loaded
            prep prep_ready cnt_saved cnt_loaded chain chain_act tables_ready
            x_loaded0 x_loaded1 stored0 stored1 blocks_final att_loaded0 att_loaded1
            td_done td_copied gates_done sig_r sig_z t_u tanh_d y_ready to_done out_done
            xc_ready ec_ready squares var_ready sd_ready norm_done xg_used
            vt_done vt_copied qk_done qk_evac scan_done st_done ms_read v_ready std_ready
            t2_done t2_copied o_done od_done t3_done t3_copied g_done sig_g gru_u tanh_g res_done
            gathered0 gathered1 scattered0 scattered1 late_made late_saved late_loaded any_late park_loaded park_index park_done index_copied index_seen""".split()
        q = {n: sem(n) for n in names}
        x_loaded, stored, att_loaded, gathered, scattered = (
            [q[n + "0"], q[n + "1"]] for n in ("x_loaded", "stored", "att_loaded", "gathered", "scattered"))

        def rows(t, start):
            return t[bass.ds(start, ROWS), :].rearrange("(p g) c -> p g c", p=P)

        loads = [
            (KR[:, :], key_r), (PR[:, :], prev_r), (AR_IN[:, :, :], attr_r), (KL[:, :], key_l), (NL[:, :], next_l),
            (KB, key_b), (GIDX[:, :], gidx), (EW[:, :], ew_l), (DH[:, :], deg_hist.partition_broadcast(P)),
            (WT2[:, 0, :], w_t), (WT2[:, 1, :], w_t),
            (WPRE[:, :, :], w_pre.rearrange("(a k) c -> k a c", k=C)), (WP0[:, :], w_post[0:C, :]),
            (WIH2[0:C, :], wih_t), (WIH2[C:P, :], wih_t), (WHH2[0:C, :], whh_t), (WHH2[C:P, :], whh_t),
            (WIHD[:, :, 0, :], wih_t.rearrange("k (g c) -> k g c", c=C)),
            (WIHD[:, :, 1, :], wih_t.rearrange("k (g c) -> k g c", c=C)),
            (WET[:, :], we_t), (WAU[AR - 1:AR, :], b_pre), (BPC[:, :], b_post),
            (BIC[0:C, :], bih_c), (BIC[C:P, :], bih_c), (BHC[0:C, :], bhh_c), (BHC[C:P, :], bhh_c),
            (BIR[:, :], bih_r), (BHR[:, :], bhh_r),
        ]
        for k in range(3):
            base = C + 4 * C * k
            cols = slice(C * k, C * k + C)
            loads += [(OW1[0:C, cols], w_post[base:base + C, :]), (OW1[C:P, cols], w_post[base + 3 * C:base + 4 * C, :]),
                      (OW2[0:C, cols], w_post[base + 2 * C:base + 3 * C, :]), (OW2[C:P, cols], w_post[base + C:base + 2 * C, :]),
                      (STDW[:, k, :], w_post[base + 3 * C:base + 4 * C, :])]
        SETUP_LOADS = 16 * len(loads)
        block = ctx.enter_context(nc.Block())

        @block.sync
        def _(sp):
            sp.dma_start(ID[:, :], ident).then_inc(q["ident_loaded"], 16)
            for to, of in loads:
                sp.dma_start(to, of).then_inc(q["setup_loaded"], 16)
            sp.dma_start(X[0][:, :, :], rows(x, 0)).then_inc(x_loaded[0], 16)
            sp.wait_ge(q["flags_made"], 1)
            sp.dma_start(keep_rows, KEEP[:, :]).then_inc(q["split_saved"], 16)
            sp.wait_ge(q["flags_made"], 2)
            sp.dma_start(attr_rows.rearrange("k p c -> p k c"), APART[:, :, :, :].rearrange("p i k c -> p (i k) c"))\
                .then_inc(q["split_saved"], 16)
            sp.wait_ge(q["flags_made"], 3)
            sp.dma_start(cnt_rows, CNT_R[:, :]).then_inc(q["cnt_saved"], 16)
            sp.wait_ge(q["cnt_saved"], 16)
            counts = cnt_rows.rearrange("p c -> (p c)").rearrange("(a t p) -> t a p", a=2, p=P)
            sp.dma_start(CNT_T[:, :, :], counts).then_inc(q["cnt_loaded"], 16)
            sp.wait_ge(q["late_made"], 1)
            sp.dma_start(late_cell, LATEI[:, :]).then_inc(q["late_saved"], 16)
            sp.wait_ge(q["late_saved"], 16)
            sp.dma_start(LATE[0:1, 0:BLOCKS], late_cell.rearrange("b a -> a b")).then_inc(q["late_loaded"], 16)
            sp.wait_ge(q["flags_made"], 4)
            sp.dma_start(wau_rows, WAUP[:, :, :]).then_inc(q["split_saved"], 16)
            sp.wait_ge(q["flags_made"], 5)
            sp.dma_start(bias_rows, BPART[:, :, :]).then_inc(q["split_saved"], 16)
            sp.wait_ge(q["split_saved"], 64)
            sp.wait_ge(q["zeroed"], 1)
            n = 0
            for j in range(PARTS):
                for i in range(PARTS):
                    at = (j * PARTS + i) * AR
                    sp.dma_start(WAUG[at:at + AR, 0:C], wau_rows[:, j, :]).then_inc(q["split_loaded"], 16)
                    n += 1
            for a in range(2):
                sp.dma_start(SBIAS[0:PARTS, a, :], bias_rows[0, :, :]).then_inc(q["split_loaded"], 16)
                n += 1
            assert n == 11

            keep_flat = keep_rows.rearrange("p c -> (p c)").rearrange("(a n) -> a n", a=1)
            attr_flat = attr_rows.rearrange("k p c -> k (p c)")

            def load_attributes(b):
                start = b.times(EB)
                start = start if isinstance(start, int) else sp.snap(start)
                wait(sp, q["qk_done"], b.next(-1).times(2))
                for j in range(PARTS):
                    sp.dma_start(ATT[b.par][j * PARTS * AR:(j + 1) * PARTS * AR, :], attr_flat[:, bass.ds(start, EB)])\
                        .then_inc(att_loaded[b.par], 16)
                sp.dma_start(ATT[b.par][KEEP_ROW:KEEP_ROW + 1, :], keep_flat[:, bass.ds(start, EB)])\
                    .then_inc(att_loaded[b.par], 16)

            load_attributes(At(None, 0))

            def step(i, more=True):
                here = i.times(STRIDE)
                here = here if isinstance(here, int) else sp.snap(here)
                if i.j is not None or i.off > 0:
                    sp.wait_ge(stored[1 - i.par], i.next(-1).pair(16))
                    sp.sem_inc(q["blocks_final"], 1)
                if more:
                    then = i.next().times(STRIDE)
                    then = then if isinstance(then, int) else sp.snap(then)
                    sp.dma_start(X[1 - i.par][:, :, :], rows(x, then)).then_inc(x_loaded[1 - i.par], 16)
                    load_attributes(i.next())
                sp.wait_ge(q["out_done"], i.times(CHUNKS, CHUNKS))
                sp.dma_start(rows(out, here), X[i.par][:, :, :]).then_inc(stored[i.par], 16)

            step(At(None, 0))
            step(At(None, 1))
            with sp.Fori(0, (BLOCKS - 3) // 2) as j:
                step(At(j, 2))
                step(At(j, 3))
            step(At(None, BLOCKS - 1), more=False)
            sp.wait_ge(stored[0], At(None, BLOCKS - 1).pair(16))
            sp.sem_inc(q["blocks_final"], 1)

        @block.gpsimd
        def _(pool):
            pool.memset(ATT[0][:, :], 0.0)
            pool.memset(ATT[1][:, :], 0.0)
            pool.memset(WAUG[:, :], 0.0)
            pool.memset(SBIAS[:, :, :], 0.0)
            pool.memset(ONESB[:, :], 1.0)
            pool.memset(SELK[:, :], 0.0)
            pool.memset(DW[:, :, :], 0.0)
            pool.memset(SW[:, :], 0.0)
            pool.memset(CARRY[:, :], 0.0)
            pool.memset(ONE[:, :], 1.0)
            pool.memset(ZERO1[:, :], 0.0).then_inc(q["zeroed"], 1)
            pool.wait_ge(q["zeroed"], 1)
            pool.affine_select(out=SELK[:, :], in_=SELK[:, :], compare_op=ALU.not_equal, fill=1.0, base=-KEEP_ROW,
                               pattern=[[0, P]], channel_multiplier=1)
            pool.iota(IDX[:, :], pattern=[[1, RC]], base=0, channel_multiplier=RC,
                      allow_small_or_imprecise_dtypes=True)
            pool.iota(LATEC[:, 1:2], pattern=[[1, 1]], base=2 * STRIDE, channel_multiplier=STRIDE,
                      allow_small_or_imprecise_dtypes=True).then_inc(q["iota_made"], 1)
            pool.wait_ge(q["setup_loaded"], SETUP_LOADS)
            pool.wait_ge(q["tables_ready"], 1)
            pool.wait_ge(q["any_late"], 1)

            bound = pool.to_reg(NODES - 1)
            any_late = pool.value_load(LATE[0:1, BLOCKS:BLOCKS + 1], min_val=0, max_val=1)

            def gather(b):
                at = b.times(2 * TILES)
                at = at if isinstance(at, int) else pool.snap(at)
                wait(pool, q["xg_used"], b.next(-1).times(1))
                pool.tensor_copy(IX[b.par][:, :], GIDX[:, bass.ds(at, 2 * TILES)]).then_inc(q["index_copied"], 1)
                wait(pool, q["index_copied"], copies(b, 0))
                pool.sem_inc(q["index_seen"], 1)
                for t in range(TILES):
                    for w in range(2):
                        pool.indirect_dma_start(
                            XG[b.par][:, t, w, :], None, x,
                            bass.IndirectOffsetOnAxis(IX[b.par][:, 2 * t + w:2 * t + w + 1], 0),
                            bounds_check=bound, oob_is_err=False).then_inc(gathered[b.par], 16)

            def copies(b, scatter):
                if scatter:
                    return b.times(2, 4)
                if b.j is None and b.off < 3:
                    return b.off + 1
                return b.times(2, -2)

            def scatter(b, last=False):
                at = b.times(TILES)
                at = at if isinstance(at, int) else pool.snap(at)
                wait(pool, scattered[b.par], b.next(-2).pair(16 * TILES))
                pool.wait_ge(q["res_done"], b.times(1, 1))
                pool.wait_ge(q["blocks_final"], BLOCKS if last else b.times(1, 2))
                pool.tensor_copy(SIX[b.par][:, :], SIDX[:, bass.ds(at, TILES)]).then_inc(q["index_copied"], 1)
                wait(pool, q["index_copied"], b.times(2, 5) if not last else b.off + BLOCKS + 1)
                pool.sem_inc(q["index_seen"], 1)
                send(b)

            def rows_to_out(index, results, done):
                for t in range(TILES):
                    pool.indirect_dma_start(
                        out, bass.IndirectOffsetOnAxis(index[:, t:t + 1], 0), results[:, t, :], None,
                        bounds_check=bound, oob_is_err=False).then_inc(done, 16)

            def send(b):
                number = b.times(1)
                number = number if isinstance(number, int) else pool.snap(number)
                with pool.If(any_late > 0):
                    pool.dma_start(parked[bass.ds(number, 1), :, :].rearrange("a p c -> p (a c)"),
                                   RES[b.par][:, :, :].rearrange("p t c -> p (t c)")).then_inc(scattered[b.par], 16)
                    pool.sem_inc(scattered[b.par], 16 * (TILES - 1))
                with pool.Else():
                    rows_to_out(SIX[b.par], RES[b.par], scattered[b.par])

            gather(At(None, 0))
            gather(At(None, 1))
            gather(At(None, 2))
            for k in range(2):
                gather(At(None, 3 + k))
                scatter(At(None, k))
            with pool.Fori(0, (BLOCKS - 5) // 2) as j:
                for k in range(2):
                    gather(At(j, 5 + k))
                    scatter(At(j, 2 + k))
            scatter(At(None, BLOCKS - 3), last=True)
            scatter(At(None, BLOCKS - 2), last=True)
            scatter(At(None, BLOCKS - 1), last=True)
            for par in range(2):
                pool.wait_ge(scattered[par], 16 * TILES * ((BLOCKS + 1 - par) // 2))
            with pool.If(any_late > 0):
                with pool.Fori(0, BLOCKS) as b:
                    at = pool.snap(b * TILES)
                    pool.tensor_copy(SIX[0][:, :], SIDX[:, bass.ds(at, TILES)]).then_inc(q["park_index"], 1)
                    pool.dma_start(RES[0][:, :, :].rearrange("p t c -> p (t c)"),
                                   parked[bass.ds(b, 1), :, :].rearrange("a p c -> p (a c)")).then_inc(q["park_loaded"], 16)
                    pool.wait_ge(q["park_index"], b + 1)
                    pool.sem_inc(q["index_seen"], 1)
                    pool.wait_ge(q["park_loaded"], b * 16 + 16)
                    pool.sem_inc(q["index_seen"], 1)
                    rows_to_out(SIX[0], RES[0], q["park_done"])
                    pool.wait_ge(q["park_done"], b * (16 * TILES) + 16 * TILES)
                    pool.sem_inc(q["index_seen"], 1)
            with pool.Else():
                pool.nop()

        @block.vector
        def _(dve):
            done = [0]
            base = [At(None, 0), 0]

            def chained(ins):
                ins.then_inc(q["chain"], 1)
                done[0] += 1

            def settle():
                dve.wait_ge(q["chain"], base[0].times(PER_STEP, base[1] + done[0]))

            def link(ins):
                chained(ins)
                settle()

            tt, ts, stt, copy = dve.tensor_tensor, dve.tensor_scalar, dve.scalar_tensor_tensor, dve.tensor_copy

            dve.wait_ge(q["setup_loaded"], SETUP_LOADS)
            dve.wait_ge(q["iota_made"], 1)
            copy(W2[:, :], KR[:, :])
            link(copy(LOC[:, :], PR[:, :]))
            link(tt(W2[:, :], W2[:, :], LOC[:, :], ALU.is_equal))
            copy(KEEP[:, :], W2[:, :]).then_inc(q["flags_made"], 1)
            ew_r = AR_IN[:, 3, :]
            for k in range(3):
                tt(AE[:, k, :], AR_IN[:, k, :], ew_r, ALU.mult)
            copy(AE[:, 3, :], ew_r)
            link(dve.memset(AE[:, 4, :], 1.0))
            for i in range(PARTS):
                link(copy(APART[:, i, :, :], AE[:, :, :]))
                if i < PARTS - 1:
                    link(tt(AE[:, :, :], AE[:, :, :], APART[:, i, :, :], ALU.subtract))
            dve.sem_inc(q["flags_made"], 1)
            link(tt(W2[:, :], W2[:, :], IDX[:, :], ALU.mult))
            link(tt(W2[:, :], IDX[:, :], W2[:, :], ALU.subtract))
            link(dve.tensor_tensor_scan(LOC[:, :], W2[:, :], W2[:, :], 0.0, ALU.max, ALU.max))
            copy(LAST[:, :], LOC[:, RC - 1:RC]).then_inc(q["prep_ready"], 1)
            dve.wait_ge(q["prep"], 1)
            link(copy(LG[0:1, 0:P], GATE[0:1, 0, 0:P]))
            link(dve.tensor_tensor_scan(CARRY[:, 1:P + 1], LG[0:1, 0:P], LG[0:1, 0:P], 0.0, ALU.max, ALU.max))
            dve.sem_inc(q["prep_ready"], 1)
            dve.wait_ge(q["prep"], 2)
            link(copy(LAST[:, :], TIN[:, 0:1]))
            link(stt(W2[:, :], LOC[:, :], LAST[:, 0:1], IDX[:, :], ALU.max, ALU.subtract))
            ts(CNT_R[:, :], W2[:, :], -1.0, 1.0, ALU.mult, ALU.add).then_inc(q["flags_made"], 1)
            copy(W0[:, :], KL[:, :])
            link(copy(W1[:, :], NL[:, :]))
            link(tt(W1[:, :], W0[:, :], W1[:, :], ALU.is_equal))
            link(stt(W1[:, :], W1[:, :], float(OUT_OF_RANGE), W0[:, :], ALU.mult, ALU.add))
            link(copy(SIDX[:, :], W1[:, :]))

            link(copy(KBF, KB))
            link(dve.tensor_reduce(LATEC[:, 0:1], KBF, AX, ALU.max))
            link(tt(LATEC[:, 2:3], LATEC[:, 0:1], LATEC[:, 1:2], ALU.is_ge))
            copy(LATEI[:, :], LATEC[:, 2:3]).then_inc(q["late_made"], 1)
            dve.wait_ge(q["late_loaded"], 16)
            dve.tensor_reduce(LATE[:, BLOCKS:BLOCKS + 1], LATE[:, 0:BLOCKS - 3], AX, ALU.max).then_inc(q["any_late"], 1)

            dve.wait_ge(q["prep"], 3)
            copy(QW[0:C, 0:C], GATE[0:C, 1, 0:C])
            ts(QW[0:C, C:P], GATE[0:C, 1, 0:C], -1.0, None, ALU.mult)
            copy(QW[C:P, 0:C], GATE[C:P, 1, C:P])
            ts(QW[C:P, C:P], GATE[C:P, 1, C:P], -1.0, None, ALU.mult)
            copy(M1D[:, 0, :], GATE[0:C, 2, 0:C])
            copy(M1D[:, 1, :], GATE[0:C, 2, 0:C])
            copy(WAU[0:4, :], GATE[0:4, 3, 0:C])
            ts(OW2[C:P, :], OW2[C:P, :], -1.0, None, ALU.mult)
            tt(BIC[:, 0:2], BIC[:, 0:2], BHC[:, 0:2], ALU.add)
            tt(BROW[:, 0:2 * C], BIR[:, 0:2 * C], BHR[:, 0:2 * C], ALU.add)
            copy(BROW[:, 2 * C:3 * C], BHR[:, 2 * C:3 * C])
            link(copy(BROW[:, 3 * C:4 * C], BIR[:, 2 * C:3 * C]))
            tt(BROW[:, 0:2 * C], BROW[:, 0:2 * C], EP[0:1, 0:2 * C], ALU.add)
            tt(BROW[:, 3 * C:4 * C], BROW[:, 3 * C:4 * C], EP[0:1, 2 * C:3 * C], ALU.add)
            dve.wait_ge(q["logs_ready"], 1)
            link(dve.tensor_reduce(AVG[:, :], LDH[:, :], AX, ALU.add))
            link(ts(AVG[:, :], AVG[:, :], 1.0 / 11, None, ALU.mult))
            dve.reciprocal(IAVG[:, :], AVG[:, :])
            link(dve.reciprocal(NOEDGE[:, 4:5], NOEDGE[:, 3:4]))
            tt(NOEDGE[:, 1:2], NOEDGE[:, 3:4], IAVG[:, :], ALU.mult)
            link(tt(NOEDGE[:, 2:3], NOEDGE[:, 4:5], AVG[:, :], ALU.mult))
            link(tt(NOEDGE[:, 2:3], NOEDGE[:, 2:3], NOEDGE[:, 1:2], ALU.mult))
            link(ts(NOEDGE[:, 1:3], NOEDGE[:, 1:3], EPS ** 0.5, None, ALU.mult))
            link(dve.memset(NOEDGE[:, 0:1], EPS ** 0.5))
            dve.sem_inc(q["prep_ready"], 1)
            for i in range(PARTS):
                link(copy(WAUP[:, i, :], WAU[:, :] if i == 0 else WAUR[:, :]))
                if i < PARTS - 1:
                    link(tt(WAUR[:, :], WAU[:, :] if i == 0 else WAUR[:, :], WAUP[:, i, :], ALU.subtract))
            dve.sem_inc(q["flags_made"], 1)
            for i in range(PARTS):
                link(copy(BPART[:, i, :], BROW[:, :] if i == 0 else BRES[:, :]))
                if i < PARTS - 1:
                    link(tt(BRES[:, :], BROW[:, :] if i == 0 else BRES[:, :], BPART[:, i, :], ALU.subtract))
            dve.sem_inc(q["flags_made"], 1)
            dve.wait_ge(q["prep"], 4)
            link(tt(BV[:, :], TOUT[0:C, 0:1], BPC[:, :], ALU.add))
            dve.sem_inc(q["prep_ready"], 1)
            for g in range(2):
                for h in range(2):
                    r = slice(C * h, C * h + C)
                    tt(DW[r, g, r], TIN[r, C * g:C * g + C], WHH2[r, C * g:C * g + C], ALU.add)
                copy(SW[C:P, C * g:C * g + C], WIH2[C:P, C * g:C * g + C])
                tt(SW[0:C, C * g:C * g + C], TIN[0:C, C * g:C * g + C], WHH2[0:C, C * g:C * g + C], ALU.add)
            for h in range(2):
                r = slice(C * h, C * h + C)
                copy(DW[r, 2, r], WHH2[r, 2 * C:3 * C])
                copy(DW[r, 3, r], TIN[r, 2 * C:3 * C])
            copy(SW[0:C, 2 * C:3 * C], WHH2[0:C, 2 * C:3 * C])
            copy(SW[0:C, 3 * C:4 * C], TIN[0:C, 2 * C:3 * C])
            link(copy(SW[C:P, 3 * C:4 * C], WIH2[C:P, 2 * C:3 * C]))
            dve.wait_ge(q["prep"], 5)
            tt(DB[:, 0:2], EP[:, 0:2], BIC[:, 0:2], ALU.add)
            copy(DB[:, 2:3], BHC[:, 2:3])
            link(tt(DB[:, 3:4], EP[:, 2:3], BIC[:, 2:3], ALU.add))
            dve.wait_ge(q["split_loaded"], 16 * 11)
            link(copy(WAUG[:, C:P], WAUG[:, 0:C]))
            link(ts(WAUG[:, C:P], WAUG[:, 0:C], -1.0, None, ALU.mult))
            dve.wait_ge(q["prep"], 6)
            copy(W0[:, 0:RC // 2], GATE[:, 0, 0:RC // 2])
            link(copy(W0[:, RC // 2:RC], GATE[:, 0, P:P + RC // 2]))
            dve.sem_inc(q["prep_ready"], 1)
            copy(COEFS[:, :, 3], EW[:, :])
            dve.reciprocal(COEFS[:, :, 0], W0[:, :])
            dve.wait_ge(q["logs_ready"], 2)
            dve.reciprocal(ILG[:, :], LG[:, :])
            link(ts(COEFS[:, :, 1], LG[:, :], IAVG[:, 0:1], None, ALU.mult))
            link(ts(ILG[:, :], ILG[:, :], AVG[:, 0:1], None, ALU.mult))
            link(tt(COEFS[:, :, 2], ILG[:, :], COEFS[:, :, 1], ALU.mult))
            dve.sem_inc(q["tables_ready"], 1)

            def spread(ap, n):
                return ap.unsqueeze(len(ap.shape)).to_broadcast(list(ap.shape) + [n])

            E0 = GROUPS
            E1 = GROUPS + 2 * TILES

            def centre(b):
                dve.wait_ge(x_loaded[b.par], b.pair(16))
                link(dve.tensor_reduce(SUM[:, 0:E0], X[b.par][:, :, :], AX, ALU.add))
                link(ts(MEAN[:, 0:E0], SUM[:, 0:E0], 1.0 / C, None, ALU.mult))
                wait(dve, q["td_done"], b.next(-1).times(CHUNKS))
                tt(XN[b.par][:, :, :], X[b.par][:, :, :], spread(MEAN[:, 0:E0], C), ALU.subtract)\
                    .then_inc(q["xc_ready"], 1)
                dve.wait_ge(gathered[b.par], b.pair(16 * 2 * TILES))
                xg = XG[b.par][:, :, :, :].rearrange("p t w c -> p (t w) c")
                link(dve.tensor_reduce(SUM[:, E0:E1], xg, AX, ALU.add))
                link(ts(MEAN[:, E0:E1], SUM[:, E0:E1], 1.0 / C, None, ALU.mult))
                tt(EC[:, :, :, :].rearrange("p t w c -> p (t w) c"), xg, spread(MEAN[:, E0:E1], C), ALU.subtract)\
                    .then_inc(q["ec_ready"], 1)

            def variance(b):
                dve.wait_ge(q["squares"], b.times(2, 1))
                dve.tensor_reduce(SSQ[:, 0:E0], SQ[:, :, :], AX, ALU.add)
                dve.wait_ge(q["squares"], b.times(2, 2))
                link(dve.tensor_reduce(SSQ[:, E0:E1], ESQ[:, :, :], AX, ALU.add))
                wait(dve, q["norm_done"], b.times(1))
                ts(VAR[:, :], SSQ[:, :], 1.0 / C, EPS, ALU.mult, ALU.add).then_inc(q["var_ready"], 1)

            def normalise(b):
                dve.wait_ge(q["sd_ready"], b.times(1, 1))
                link(dve.reciprocal(RSTD[:, :], VAR[:, :]))
                link(tt(XN[b.par][:, :, :], XN[b.par][:, :, :], spread(RSTD[:, 0:E0], C), ALU.mult))
                at = b.times(TILES)
                at = at if isinstance(at, int) else dve.snap(at)
                ts(COEF[b.par][:, :, :], COEFS[:, bass.ds(at, TILES), :], 1.0, None, ALU.mult)
                rs = RSTD[:, E0:E1].rearrange("p (t w) -> p t w", w=2)
                stt(HO[b.par][:, :, 0:C], EC[:, :, 0, :], 0.0, spread(rs[:, :, 0], C), ALU.max, ALU.mult)
                link(stt(HS[:, :, :], EC[:, :, 1, :], 0.0, spread(rs[:, :, 1], C), ALU.max, ALU.mult))
                copy(XD[b.par][:, :, :], XG[b.par][:, :, 0, :]).then_inc(q["xg_used"], 1)
                wait(dve, q["vt_done"], b.times(1))
                ew = spread(COEF[b.par][:, :, 3], C)
                tt(V[:, :, 0:C], HO[b.par][:, :, 0:C], ew, ALU.mult)
                tt(V[:, :, C:P], HS[:, :, :], ew, ALU.mult).then_inc(q["norm_done"], 1)

            def gate_n(i, c):
                dve.wait_ge(q["sig_r"], i.times(CHUNKS, c + 1))
                dve.wait_ge(q["gates_done"], i.times(4 * CHUNKS, 4 * c + 3))
                link(stt(T[:, :], GATE[:, 2, :], DB[:, 2:3], SR[c % 2][:, :], ALU.add, ALU.mult))
                dve.wait_ge(q["gates_done"], i.times(4 * CHUNKS, 4 * c + 4))
                wait(dve, q["tanh_d"], i.times(CHUNKS, c - 1))
                tt(U[c % 2][:, :], T[:, :], GATE[:, 3, :], ALU.add).then_inc(q["t_u"], 1)

            def mix(i, c):
                dve.wait_ge(q["tanh_d"], i.times(CHUNKS, c + 1))
                link(tt(D[:, :], HT[c % 2][:, :], NN[c % 2][:, :], ALU.subtract))
                dve.wait_ge(q["sig_z"], i.times(CHUNKS, c + 1))
                link(tt(D[:, :], D[:, :], SZ[c % 2][:, :], ALU.mult))
                wait(dve, q["to_done"], i.times(CHUNKS, c - 1))
                tt(Y[c % 2][:, :], D[:, :], NN[c % 2][:, :], ALU.add).then_inc(q["y_ready"], 1)

            def add_x(i, c):
                dve.wait_ge(q["to_done"], i.times(CHUNKS, c + 1))
                xs = X[i.par][:, GC * c:GC * c + GC, :].rearrange("p g c -> p (g c)")
                tt(xs, xs, TOUT[:, :], ALU.add).then_inc(q["out_done"], 1)

            def scan(i, h):
                cols = slice(HALF * h, HALF * h + HALF)
                dve.wait_ge(q["qk_evac"], i.times(2, h + 1))
                wait(dve, q["st_done"], i.times(1))
                wait(dve, q["o_done"], i.next(-1).times(2))
                first = h == 0 and i.j is None and i.off == 0
                before = EB - 1 if h == 0 else HALF - 1
                s0 = 0.0 if first else S[:, before:before + 1]
                m0 = -BIG if first else MX[i.par if h else 1 - i.par][:, before:before + 1]
                dve.tensor_tensor_scan(S[:, cols], EP[:, HALF:EB], H[:, :], s0, ALU.mult, ALU.add)
                dve.tensor_tensor_scan(MX[i.par][:, cols], CAP[:, :], EP[:, 0:HALF], m0, ALU.min, ALU.max)\
                    .then_inc(q["scan_done"], 1)

            def moments(i):
                dve.wait_ge(q["st_done"], i.times(1, 1))
                wait(dve, q["t2_done"], i.times(1))
                tt(MS[:, :, :], EPT, spread(COEF[i.par][:, :, 0], P), ALU.mult).then_inc(q["ms_read"], 1)
                dve.wait_ge(q["ms_read"], i.times(1, 1))
                link(tt(M2[:, :, :], MS[:, :, 0:C], MS[:, :, 0:C], ALU.mult))
                link(tt(MS[:, :, C:P], MS[:, :, C:P], M2[:, :, :], ALU.subtract))
                ts(MS[:, :, C:P], MS[:, :, C:P], 0.0, EPS, ALU.max, ALU.add).then_inc(q["v_ready"], 1)

            def post(b, h):
                tiles = slice(TH * h, TH * h + TH)
                dve.wait_ge(q["o_done"], b.times(2, h + 1))
                t1 = T1[:, :, :].rearrange("p t (k c) -> p t k c", k=2)
                scalers = spread(COEF[b.par][:, tiles, 1:3], C)
                link(tt(t1, EPW[:, :, C:3 * C].rearrange("p t (k c) -> p t k c", k=2), scalers, ALU.mult))
                link(tt(OS[:, :, :], T1[:, :, 0:C], T1[:, :, C:P], ALU.add))
                tt(HO[b.par][:, tiles, C:P], OS[:, :, :], EPW[:, :, 0:C], ALU.add).then_inc(q["od_done"], 1)

            def edge_gate_n(b, h):
                tiles = slice(TH * h, TH * h + TH)
                dve.wait_ge(q["sig_g"], b.times(2, h + 1))
                link(tt(TG[:, :, :], EPW[:, :, 2 * C:3 * C], RZ[:, tiles, 0:C], ALU.mult))
                tt(UG[:, tiles, :], TG[:, :, :], EPW[:, :, 3 * C:4 * C], ALU.add).then_inc(q["gru_u"], 1)

            def edge_mix(b):
                dve.wait_ge(q["tanh_g"], b.times(2, 2))
                wait(dve, scattered[b.par], b.next(-2).pair(16 * TILES)) if b.j is not None or b.off > 1 else None
                link(tt(DG[:, :, :], HO[b.par][:, :, 0:C], NG[:, :, :], ALU.subtract))
                link(tt(DG[:, :, :], DG[:, :, :], RZ[:, :, C:P], ALU.mult))
                link(tt(DG[:, :, :], DG[:, :, :], NG[:, :, :], ALU.add))
                tt(RES[b.par][:, :, :], DG[:, :, :], XD[b.par][:, :, :], ALU.add).then_inc(q["res_done"], 1)

            def step(i, new=True, old=True):
                p = i.next(-1)
                done[0] = 0
                gate_n(i, 0)
                scan(i, 0)
                mix(i, 0)
                if old:
                    post(p, 0)
                gate_n(i, 1)
                add_x(i, 0)
                scan(i, 1)
                mix(i, 1)
                if old:
                    post(p, 1)
                gate_n(i, 2)
                add_x(i, 1)
                moments(i)
                mix(i, 2)
                if new:
                    centre(i.next())
                gate_n(i, 3)
                add_x(i, 2)
                if old:
                    edge_gate_n(p, 0)
                mix(i, 3)
                if old:
                    edge_gate_n(p, 1)
                if new:
                    variance(i.next())
                add_x(i, 3)
                if old:
                    edge_mix(p)
                if new:
                    normalise(i.next())

            centre(At(None, 0))
            variance(At(None, 0))
            normalise(At(None, 0))
            base[1] = done[0]
            step(At(None, 0), old=False)
            at_one = base[1] + done[0]
            base[:] = [At(None, 1), at_one - PER_STEP]
            step(At(None, 1))
            assert done[0] == PER_STEP, done[0]
            with dve.Fori(0, (BLOCKS - 3) // 2) as j:
                for k in range(2):
                    base[0] = At(j, 2 + k)
                    step(At(j, 2 + k))
            base[0] = At(None, BLOCKS - 1)
            step(At(None, BLOCKS - 1), new=False)
            last = At(None, BLOCKS - 1)
            post(last, 0)
            post(last, 1)
            edge_gate_n(last, 0)
            edge_gate_n(last, 1)
            edge_mix(last)

        @block.scalar
        def _(act):
            def act_on(out_, in_, func, **kw):
                return act.activation(out_, in_, func, **kw)

            act.wait_ge(q["setup_loaded"], SETUP_LOADS)
            act.wait_ge(q["zeroed"], 1)
            act_on(LDH[:, :], DH[:, :], ACT.Ln, bias=ONE[:, 0:1])
            act_on(NOEDGE[:, 3:4], ONE[:, :], ACT.Ln, bias=ONE[:, 0:1]).then_inc(q["logs_ready"], 1)
            act.wait_ge(q["prep_ready"], 5)
            act_on(LG[:, :], W0[:, :], ACT.Ln, bias=ONE[:, 0:1]).then_inc(q["logs_ready"], 1)

            def squares(b):
                act.wait_ge(q["xc_ready"], b.times(1, 1))
                wait(act, q["var_ready"], b.times(1))
                act_on(SQ[:, :, :], XN[b.par][:, :, :], ACT.Square).then_inc(q["squares"], 1)
                act.wait_ge(q["ec_ready"], b.times(1, 1))
                act_on(ESQ[:, :, :], EC[:, :, :, :].rearrange("p t w c -> p (t w) c"), ACT.Square)\
                    .then_inc(q["squares"], 1)

            def roots(i, new=True, cur=True):
                if cur:
                    act.wait_ge(q["v_ready"], i.times(1, 1))
                    act_on(MS[:, :, C:P], MS[:, :, C:P], ACT.Sqrt).then_inc(q["std_ready"], 1)
                if new:
                    b = i.next()
                    act.wait_ge(q["var_ready"], b.times(1, 1))
                    act_on(VAR[:, :], VAR[:, :], ACT.Sqrt).then_inc(q["sd_ready"], 1)

            def take_h(i, c):
                act.wait_ge(q["td_done"], i.times(CHUNKS, c + 1))
                wait(act, q["gates_done"], i.times(4 * CHUNKS, 4 * (c - 1)))
                wait(act, q["y_ready"], i.times(CHUNKS, c - 1))
                act_on(HT[c % 2][:, :], TIN[:, :], ACT.Relu).then_inc(q["td_copied"], 1)

            def gates_rz(i, c):
                act.wait_ge(q["gates_done"], i.times(4 * CHUNKS, 4 * c + 1))
                wait(act, q["t_u"], i.times(CHUNKS, c - 1))
                act_on(SR[c % 2][:, :], GATE[:, 0, :], ACT.Sigmoid, bias=DB[:, 0:1]).then_inc(q["sig_r"], 1)
                act.wait_ge(q["gates_done"], i.times(4 * CHUNKS, 4 * c + 2))
                wait(act, q["y_ready"], i.times(CHUNKS, c - 1))
                act_on(SZ[c % 2][:, :], GATE[:, 1, :], ACT.Sigmoid, bias=DB[:, 1:2]).then_inc(q["sig_z"], 1)

            def gate_n(i, c):
                act.wait_ge(q["t_u"], i.times(CHUNKS, c + 1))
                wait(act, q["y_ready"], i.times(CHUNKS, c - 1))
                act_on(NN[c % 2][:, :], U[c % 2][:, :], ACT.Tanh, bias=DB[:, 3:4]).then_inc(q["tanh_d"], 1)

            def messages(i, h):
                act.wait_ge(q["qk_done"], i.times(2, h + 1))
                wait(act, q["scan_done"], i.times(2, h))
                act_on(H[0:C, :], EP[0:C, 0:HALF], ACT.Copy)
                act_on(H[C:P, :], EP[C:P, 0:HALF], ACT.Square)
                act_on(CAP[:, :], EP[:, HALF:EB], ACT.Copy, scale=2 * BIG, bias=-BIG).then_inc(q["qk_evac"], 1)

            def edge_gates_rz(b, h):
                tiles = slice(TH * h, TH * h + TH)
                act.wait_ge(q["g_done"], b.times(2, h + 1))
                wait(act, q["res_done"], b.times(1))
                act_on(RZ[:, tiles, :], EPW[:, :, 0:2 * C], ACT.Sigmoid).then_inc(q["sig_g"], 1)

            def edge_gate_n(b, h):
                tiles = slice(TH * h, TH * h + TH)
                act.wait_ge(q["gru_u"], b.times(2, h + 1))
                act_on(NG[:, tiles, :], UG[:, tiles, :], ACT.Tanh).then_inc(q["tanh_g"], 1)

            def take_v(i):
                act.wait_ge(q["vt_done"], i.times(1, 1))
                wait(act, q["qk_done"], i.times(2))
                act_on(VTS[:, :], EP[:, :], ACT.Copy).then_inc(q["vt_copied"], 1)

            def take_moments(b):
                act.wait_ge(q["t2_done"], b.times(1, 1))
                wait(act, q["o_done"], b.times(2))
                act_on(MST[:, :], EP[:, :], ACT.Copy).then_inc(q["t2_copied"], 1)

            def take_ho(b):
                act.wait_ge(q["t3_done"], b.times(1, 1))
                wait(act, q["g_done"], b.times(2))
                act_on(HOT[:, :], EP[:, :], ACT.Copy).then_inc(q["t3_copied"], 1)

            def step(i, new=True, old=True):
                p = i.next(-1)
                take_h(i, 0)
                take_v(i)
                if old:
                    take_moments(p)
                gates_rz(i, 0)
                take_h(i, 1)
                messages(i, 0)
                gate_n(i, 0)
                gates_rz(i, 1)
                take_h(i, 2)
                messages(i, 1)
                gate_n(i, 1)
                gates_rz(i, 2)
                take_h(i, 3)
                if old:
                    take_ho(p)
                gate_n(i, 2)
                if new:
                    squares(i.next())
                gates_rz(i, 3)
                if old:
                    edge_gates_rz(p, 0)
                gate_n(i, 3)
                if old:
                    edge_gate_n(p, 0)
                    edge_gates_rz(p, 1)
                    edge_gate_n(p, 1)
                roots(i, new)

            squares(At(None, 0))
            roots(At(None, -1), cur=False)
            step(At(None, 0), old=False)
            step(At(None, 1))
            with act.Fori(0, (BLOCKS - 3) // 2) as j:
                step(At(j, 2))
                step(At(j, 3))
            last = At(None, BLOCKS - 1)
            step(last, new=False)
            take_moments(last)
            take_ho(last)
            for h in range(2):
                edge_gates_rz(last, h)
                edge_gate_n(last, h)

        @block.tensor
        def _(pe):
            mm, tr = pe.matmul, pe.transpose
            pe.wait_ge(q["ident_loaded"], 16)
            pe.wait_ge(q["setup_loaded"], SETUP_LOADS)
            pe.wait_ge(q["prep_ready"], 1)
            mm(GATE[0:1, 0, 0:P], LAST[:, :], ID[:, :], start=True, stop=True).then_inc(q["prep"], 1)
            pe.wait_ge(q["zeroed"], 1)
            pe.wait_ge(q["prep_ready"], 2)
            mm(TIN[:, 0:1], CARRY[0:1, 0:P], ONE[0:1, 0:1], start=True, stop=True).then_inc(q["prep"], 1)
            mm(GATE[:, 1, 0:P], WT2[:, :, :].rearrange("k a c -> k (a c)"),
               WPRE[:, 0:2, :].rearrange("k a c -> k (a c)"), start=True, stop=True)
            mm(GATE[0:C, 2, 0:C], WP0[:, :], WT2[:, 0, :], start=True, stop=True)
            mm(GATE[0:4, 3, 0:C], WET[:, :], WPRE[:, 2, :], start=True, stop=True)
            mm(EP[0:1, 0:3 * C], BPC[:, :], WIH2[0:C, :], start=True, stop=True).then_inc(q["prep"], 1)
            pe.wait_ge(q["prep_ready"], 3)
            mm(TIN[:, 0:3 * C], M1D[:, :, :].rearrange("k a c -> k (a c)"), WIH2[0:C, :], start=True, stop=True)
            for k in range(3):
                last = mm(TOUT[0:C, 0:1], STDW[:, k, :], NOEDGE[0:C, k:k + 1], start=k == 0, stop=k == 2)
            last.then_inc(q["prep"], 1)
            pe.wait_ge(q["prep_ready"], 4)
            for g in range(3):
                last = mm(EP[:, g:g + 1], WIHD[:, g, :, :].rearrange("k a c -> k (a c)"), BV[:, :], start=True, stop=True)
            last.then_inc(q["prep"], 1)
            pe.wait_ge(q["cnt_loaded"], 16)
            half = RC // 2
            tr(GATE[:, 0, 0:half], CNT_T[:, 0, :], ID[0:half, 0:half])
            tr(GATE[:, 0, P:P + half], CNT_T[:, 1, :], ID[0:half, 0:half]).then_inc(q["prep"], 1)
            pe.wait_ge(q["tables_ready"], 1)

            def rows_in(i, c):
                pe.wait_ge(q["norm_done"], i.times(1, 1))
                wait(pe, q["td_copied"], i.times(CHUNKS, c))
                for k in range(4):
                    g = GC * c + 2 * k
                    last = tr(TIN[:, P * k:P * k + P], XN[i.par][:, g:g + 2, :].rearrange("p g c -> p (g c)"), ID[:, :])
                last.then_inc(q["td_done"], 1)

            def gates(i, c):
                pe.wait_ge(q["td_copied"], i.times(CHUNKS, c + 1))
                for g, free in enumerate((q["sig_r"], q["sig_z"], q["t_u"], q["t_u"])):
                    wait(pe, free, i.times(CHUNKS, c))
                    mm(GATE[:, g, :], DW[:, g, :], HT[c % 2][:, :], start=True, stop=True).then_inc(q["gates_done"], 1)

            def rows_out(i, c):
                pe.wait_ge(q["y_ready"], i.times(CHUNKS, c + 1))
                wait(pe, q["out_done"], i.times(CHUNKS, c))
                for k in range(4):
                    last = tr(TOUT[:, P * k:P * k + P], Y[c % 2][:, P * k:P * k + P], ID[:, :])
                last.then_inc(q["to_done"], 1)

            def tiles_turned(of, done_):
                for t in range(TILES):
                    last = tr(EPT[:, t, :], of[:, t, :], ID[:, :])
                last.then_inc(done_, 1)

            def turn_v(i):
                wait(pe, q["gru_u"], i.next(-1).times(2))
                tiles_turned(V, q["vt_done"])

            def turn_moments(b):
                pe.wait_ge(q["vt_copied"], b.times(1, 2) if b.j is not None or b.off < BLOCKS - 1 else BLOCKS)
                pe.wait_ge(q["std_ready"], b.times(1, 1))
                tiles_turned(MS, q["t2_done"])

            def messages(i, h):
                if h == 0:
                    pe.wait_ge(q["vt_copied"], i.times(1, 1))
                    wait(pe, q["t2_copied"], i.times(1))
                    pe.wait_ge(att_loaded[i.par], i.pair(16 * (PARTS + 1)))
                else:
                    wait(pe, q["od_done"], i.next(-1).times(2, 1))
                    pe.wait_ge(q["scan_done"], i.times(2, 1))
                cols = slice(HALF * h, HALF * h + HALF)
                att = ATT[i.par][:, cols]
                mm(EP[:, 0:HALF], QW[:, :], VTS[:, cols], start=True, stop=False)
                mm(EP[:, 0:HALF], WAUG[:, :], att, start=False, stop=True)
                mm(EP[:, HALF:EB], SELK[:, :], att, start=True, stop=True).then_inc(q["qk_done"], 1)

            def post(b, h, scans):
                pe.wait_ge(q["t2_copied"], b.times(1, 1))
                if scans is not None:
                    pe.wait_ge(q["scan_done"], scans.times(2, h + 1))
                elif h:
                    pe.wait_ge(q["od_done"], b.times(2, 1))
                for t in range(TH):
                    cols = slice(HALF * h + P * t, HALF * h + P * t + P)
                    mm(EPW[:, t, 0:3 * C], MST[:, cols], OW1[:, :], start=True, stop=False)
                    last = mm(EPW[:, t, 0:3 * C], MX[b.par][:, cols], OW2[:, :], start=False, stop=True)
                last.then_inc(q["o_done"], 1)

            def turn_sums(i):
                wait(pe, q["od_done"], i.times(2))
                pe.wait_ge(q["scan_done"], i.times(2, 2))
                for t in range(TILES):
                    last = tr(EPT[:, t, :], S[:, P * t:P * t + P], ID[:, :])
                last.then_inc(q["st_done"], 1)

            def turn_ho(b, sums):
                if sums is not None:
                    pe.wait_ge(q["ms_read"], sums.times(1, 1))
                pe.wait_ge(q["od_done"], b.times(2, 2))
                tiles_turned(HO[b.par], q["t3_done"])

            def edge_gates(b, h):
                pe.wait_ge(q["t3_copied"], b.times(1, 1))
                if h:
                    pe.wait_ge(q["gru_u"], b.times(2, 1))
                for a in range(2):
                    mm(EP[:, HALF * a:HALF * a + HALF], ONESB[:, :], SBIAS[:, :, :].rearrange("p a c -> p (a c)"),
                       start=True, stop=False, skip_group_check=True)
                    for t in (2 * a, 2 * a + 1):
                        cols = slice(HALF * h + P * t, HALF * h + P * t + P)
                        last = mm(EPW[:, t, :], HOT[:, cols], SW[:, :], start=False, stop=t % 2 == 1, skip_group_check=True)
                last.then_inc(q["g_done"], 1)

            def step(i, old=True):
                p = i.next(-1)
                rows_in(i, 0)
                turn_v(i)
                if old:
                    turn_moments(p)
                rows_in(i, 1)
                gates(i, 0)
                messages(i, 0)
                rows_in(i, 2)
                gates(i, 1)
                if old:
                    post(p, 0, i)
                rows_out(i, 0)
                messages(i, 1)
                rows_in(i, 3)
                gates(i, 2)
                if old:
                    post(p, 1, i)
                rows_out(i, 1)
                turn_sums(i)
                gates(i, 3)
                if old:
                    turn_ho(p, i)
                rows_out(i, 2)
                if old:
                    edge_gates(p, 0)
                    edge_gates(p, 1)
                rows_out(i, 3)

            step(At(None, 0), old=False)
            step(At(None, 1))
            with pe.Fori(0, (BLOCKS - 3) // 2) as j:
                step(At(j, 2))
                step(At(j, 3))
            last = At(None, BLOCKS - 1)
            step(last)
            pe.wait_ge(q["ms_read"], BLOCKS)
            pe.wait_ge(q["gru_u"], 2 * (BLOCKS - 1))
            turn_moments(last)
            post(last, 0, None)
            post(last, 1, None)
            turn_ho(last, None)
            edge_gates(last, 0)
            edge_gates(last, 1)




def kernel(x, src, dst, edge_attr_4, L0_gnn_deg_hist, L0_gnn_weight, L0_gnn_W_e, L0_gnn_b_e, L0_gnn_W_pre, L0_gnn_b_pre,
           L0_gnn_W_post, L0_gnn_b_post, L0_gnn_W_ih, L0_gnn_W_hh, L0_gnn_b_ih, L0_gnn_b_hh):
    import numpy as np
    import concourse.bacc as bacc
    from concourse.bass_utils import run_bass_kernel_spmd

    x, src, dst, attr = (np.asarray(a) for a in (x, src, dst, edge_attr_4))
    pad = EDGES_PADDED - EDGES

    def padded(a, value):
        return np.concatenate([a, np.full((pad,) + a.shape[1:], value, a.dtype)])

    def by_tile(a):
        return a.reshape(ALL_TILES, P).T

    key = padded(dst, NODES)
    ends = np.full(1, NODES, dst.dtype), np.full(1, -1, dst.dtype)
    gidx = np.stack([by_tile(padded(dst, 0)), by_tile(padded(src, 0))], axis=2).reshape(P, 2 * ALL_TILES)
    attr = padded(attr, 0)
    w_ih, w_hh = np.asarray(L0_gnn_W_ih), np.asarray(L0_gnn_W_hh)
    b_ih, b_hh = np.asarray(L0_gnn_b_ih), np.asarray(L0_gnn_b_hh)
    arrays = {
        "x": x, "gidx": gidx, "key_l": by_tile(key), "next_l": by_tile(np.concatenate([key[1:], ends[0]])),
        "key_r": key.reshape(P, RC), "prev_r": np.concatenate([ends[1], key[:-1]]).reshape(P, RC),
        "key_b": key.reshape(BLOCKS, EB), "attr_r": attr.T.reshape(4, P, RC).transpose(1, 0, 2),
        "ew_l": by_tile(attr[:, 3]), "ident": np.eye(P, dtype=np.float32),
        "w_t": np.asarray(L0_gnn_weight)[0].T, "w_pre": np.asarray(L0_gnn_W_pre), "w_post": np.asarray(L0_gnn_W_post),
        "wih_t": w_ih.T, "whh_t": w_hh.T,
        "we_t": np.concatenate([np.asarray(L0_gnn_W_e), np.asarray(L0_gnn_b_e)[None]]).T,
        "b_pre": np.asarray(L0_gnn_b_pre)[None], "b_post": np.asarray(L0_gnn_b_post)[:, None],
        "bih_c": b_ih.reshape(3, C).T, "bhh_c": b_hh.reshape(3, C).T, "bih_r": b_ih[None], "bhh_r": b_hh[None],
        "deg_hist": np.asarray(L0_gnn_deg_hist),
    }
    arrays = {k: np.ascontiguousarray(v) for k, v in arrays.items()}
    nc = bacc.Bacc("TRN2", target_bir_lowering=False, num_devices=1)
    args = {k: nc.dram_tensor("in_" + k, v.shape, mybir.dt.from_np(v.dtype), kind="ExternalInput").ap()
            for k, v in arrays.items()}
    out = nc.dram_tensor("out", (NODES, C), mybir.dt.float32, kind="ExternalOutput").ap()
    gnn_kernel(nc, out=out, **args)
    r = run_bass_kernel_spmd(nc, [{"in_" + k: v for k, v in arrays.items()}], core_ids=[0])
    return r.results[0]["out"]
```

```python
import concourse.bass as bass
from concourse import mybir
from contextlib import ExitStack

NODES, C, EDGES = 100000, 64, 25000
P = 128
BLOCKS = 25
GROUPS = 32
ROWS = P * GROUPS
STRIDE = (NODES - ROWS) // (BLOCKS - 1)
CHUNKS = 4
GC = GROUPS // CHUNKS
TILES = 8
EB = P * TILES
HALF = EB // 2
TH = TILES // 2
ALL_TILES = BLOCKS * TILES
EDGES_PADDED = BLOCKS * EB
RC = EDGES_PADDED // P
OUT_OF_RANGE = 1 << 20
BIG = 1.5e38
EPS = 1e-5
PARTS = 3
AR = 5
KEEP_ROW = PARTS * PARTS * AR
PER_STEP = 28
assert STRIDE * (BLOCKS - 1) + ROWS == NODES and EDGES <= EDGES_PADDED


class At:

    def __init__(self, j, off):
        self.j, self.off = j, off

    def times(self, per, plus=0):
        c = per * self.off + plus
        return c if self.j is None else self.j * (2 * per) + c

    def pair(self, per):
        c = per * (self.off // 2 + 1)
        return c if self.j is None else self.j * per + c

    def next(self, n=1):
        return At(self.j, self.off + n)

    @property
    def par(self):
        return self.off % 2


def wait(e, sem, value):
    if isinstance(value, int) and value <= 0:
        return
    e.wait_ge(sem, value)


def gnn_kernel(nc, x, gidx, key_l, next_l, key_r, prev_r, key_b, attr_r, ew_l, ident, w_t, w_pre, w_post,
               wih_t, whh_t, we_t, b_pre, b_post, bih_c, bhh_c, bih_r, bhh_r, deg_hist, out):
    f32, bf16, i32 = mybir.dt.float32, mybir.dt.bfloat16, mybir.dt.int32
    ALU, ACT, AX = mybir.AluOpType, mybir.ActivationFunctionType, mybir.AxisListType.X

    ctx = ExitStack()
    with ctx:
        def sb(name, shape, dt=f32):
            return ctx.enter_context(nc.sbuf_tensor(name, shape, dt))

        def pb(name, shape):
            return ctx.enter_context(nc.psum_tensor(name, shape, f32))

        def sem(name):
            return ctx.enter_context(nc.semaphore(name))

        cnt_rows = nc.dram_tensor("cnt_rows", (P, RC), f32, kind="Internal").ap()
        keep_rows = nc.dram_tensor("keep_rows", (P, RC), bf16, kind="Internal").ap()
        attr_rows = nc.dram_tensor("attr_rows", (PARTS * AR, P, RC), bf16, kind="Internal").ap()
        wau_rows = nc.dram_tensor("wau_rows", (AR, PARTS, C), bf16, kind="Internal").ap()
        late_cell = nc.dram_tensor("late_cell", (BLOCKS, 1), i32, kind="Internal").ap()
        parked = nc.dram_tensor("parked", (BLOCKS, P, TILES * C), f32, kind="Internal").ap()
        bias_rows = nc.dram_tensor("bias_rows", (1, PARTS, 4 * C), bf16, kind="Internal").ap()

        GIDX = sb("GIDX", [P, ALL_TILES * 2], i32)
        SIDX = sb("SIDX", [P, ALL_TILES], i32)
        COEFS = sb("COEFS", [P, ALL_TILES, 4])
        ID = sb("ID", [P, P])
        DW = sb("DW", [P, 4, P])
        DB = sb("DB", [P, 4])
        QW = sb("QW", [P, P])
        WAUG = sb("WAUG", [P, P], bf16)
        SELK = sb("SELK", [P, P], bf16)
        OW1 = sb("OW1", [P, 3 * C])
        OW2 = sb("OW2", [P, 3 * C])
        SW = sb("SW", [P, 4 * C])
        SBIAS = sb("SBIAS", [P, 2, 4 * C], bf16)
        ONESB = sb("ONESB", [P, P], bf16)
        ATT = [sb(f"ATT{i}", [P, EB], bf16) for i in range(2)]

        X = [sb(f"X{i}", [P, GROUPS, C]) for i in range(2)]
        XN = [sb(f"XN{i}", [P, GROUPS, C]) for i in range(2)]
        SQ = sb("SQ", [P, GROUPS, C])
        HT = [sb(f"HT{i}", [P, 512]) for i in range(2)]
        SR = [sb(f"SR{i}", [P, 512]) for i in range(2)]
        SZ = [sb(f"SZ{i}", [P, 512]) for i in range(2)]
        T = sb("T", [P, 512])
        U = [sb(f"U{i}", [P, 512]) for i in range(2)]
        NN = [sb(f"NN{i}", [P, 512]) for i in range(2)]
        D = sb("D", [P, 512])
        Y = [sb(f"Y{i}", [P, 512]) for i in range(2)]
        SUM = sb("SUM", [P, GROUPS + 2 * TILES])
        MEAN = sb("MEAN", [P, GROUPS + 2 * TILES])
        SSQ = sb("SSQ", [P, GROUPS + 2 * TILES])
        VAR = sb("VAR", [P, GROUPS + 2 * TILES])
        RSTD = sb("RSTD", [P, GROUPS + 2 * TILES])

        IX = [sb(f"IX{i}", [P, 2 * TILES], i32) for i in range(2)]
        XG = [sb(f"XG{i}", [P, TILES, 2, C]) for i in range(2)]
        EC = sb("EC", [P, TILES, 2, C])
        ESQ = sb("ESQ", [P, TILES * 2, C])
        RW = sb("RW", [P, TILES, 2])
        V = sb("V", [P, TILES, 2 * C])
        HO = [sb(f"HO{i}", [P, TILES, 2 * C]) for i in range(2)]
        XD = [sb(f"XD{i}", [P, TILES, C]) for i in range(2)]
        COEF = [sb(f"COEF{i}", [P, TILES, 4]) for i in range(2)]
        VTS = sb("VTS", [P, EB])
        H = sb("H", [P, HALF])
        CAP = sb("CAP", [P, HALF])
        S = sb("S", [P, EB])
        MX = [sb(f"MX{i}", [P, EB]) for i in range(2)]
        MS = sb("MS", [P, TILES, 2 * C])
        M2 = sb("M2", [P, TILES, C])
        MST = sb("MST", [P, EB])
        T1 = sb("T1", [P, TH, 2 * C])
        OS = sb("OS", [P, TH, C])
        HOT = sb("HOT", [P, EB])
        RZ = sb("RZ", [P, TILES, 2 * C])
        TG = sb("TG", [P, TH, C])
        UG = sb("UG", [P, TILES, C])
        NG = sb("NG", [P, TILES, C])
        DG = sb("DG", [P, TILES, C])
        RES = [sb(f"RES{i}", [P, TILES, C]) for i in range(2)]
        SIX = [sb(f"SIX{i}", [P, TILES], i32) for i in range(2)]

        TIN = pb("TIN", [P, 512])
        TOUT = pb("TOUT", [P, 512])
        GATE = pb("GATE", [P, 4, 512])
        EP = pb("EP", [P, EB])
        EPT = EP[:, :].rearrange("p (t c) -> p t c", c=2 * C)
        EPW = EP[:, :].rearrange("p (t c) -> p t c", c=4 * C)

        KL = sb("KL", [P, ALL_TILES], i32)
        NL = sb("NL", [P, ALL_TILES], i32)
        KR = sb("KR", [P, RC], i32)
        PR = sb("PR", [P, RC], i32)
        spare = XN[1][:, :, :].rearrange("p g c -> p (g c)")
        AR_IN = spare[:, 0:4 * RC].rearrange("p (k c) -> p k c", k=4)
        EW = sb("EW", [P, ALL_TILES])
        W0 = sb("W0", [P, ALL_TILES])
        W1 = sb("W1", [P, ALL_TILES])
        W2 = sb("W2", [P, ALL_TILES])
        LATE = sb("LATE", [1, BLOCKS + 1], i32)
        LATEC = sb("LATEC", [BLOCKS, 4])
        LATEI = sb("LATEI", [BLOCKS, 1], i32)
        KB = SQ[0:BLOCKS, :, :].rearrange("p g c -> p (g c)")[:, 0:EB].bitcast(i32)
        KBF = SQ[0:BLOCKS, :, :].rearrange("p g c -> p (g c)")[:, EB:2 * EB]
        IDX = sb("IDX", [P, RC])
        KEEP = sb("KEEP", [P, RC], bf16)
        LOC = sb("LOC", [P, RC])
        CARRY = sb("CARRY", [1, P + 1])
        LAST = sb("LAST", [P, 1])
        CNT_R = sb("CNT_R", [P, RC])
        CNT_T = sb("CNT_T", [RC // 2, 2, P])
        AE = spare[:, 4 * RC:(4 + AR) * RC].rearrange("p (k c) -> p k c", k=AR)
        APART = X[1][:, :, :].rearrange("p g c -> p (g c)").bitcast(bf16)[:, 0:PARTS * AR * RC]\
            .rearrange("p (i k c) -> p i k c", i=PARTS, k=AR)
        ONE = sb("ONE", [P, 1])
        ZERO1 = sb("ZERO1", [P, 1])
        WT2 = sb("WT2", [C, 2, C])
        WPRE = sb("WPRE", [C, 3, C])
        WP0 = sb("WP0", [C, C])
        STDW = sb("STDW", [C, 3, C])
        WIHD = sb("WIHD", [C, 3, 2, C])
        WIH2 = sb("WIH2", [P, 3 * C])
        WHH2 = sb("WHH2", [P, 3 * C])
        WET = sb("WET", [C, 4])
        WAU = sb("WAU", [AR, C])
        WAUR = sb("WAUR", [AR, C])
        WAUP = sb("WAUP", [AR, PARTS, C], bf16)
        BPC = sb("BPC", [C, 1])
        BV = sb("BV", [C, 1])
        BIC = sb("BIC", [P, 3])
        BHC = sb("BHC", [P, 3])
        BIR = sb("BIR", [1, 3 * C])
        BHR = sb("BHR", [1, 3 * C])
        BROW = sb("BROW", [1, 4 * C])
        BRES = sb("BRES", [1, 4 * C])
        BPART = sb("BPART", [1, PARTS, 4 * C], bf16)
        DH = sb("DH", [P, 11])
        LDH = sb("LDH", [P, 11])
        AVG = sb("AVG", [P, 1])
        IAVG = sb("IAVG", [P, 1])
        LG = sb("LG", [P, ALL_TILES])
        ILG = sb("ILG", [P, ALL_TILES])
        NOEDGE = sb("NOEDGE", [P, 8])
        M1D = sb("M1D", [C, 2, C])

        names = """setup_loaded ident_loaded zeroed flags_made iota_made logs_ready split_saved split_loaded
            prep prep_ready cnt_saved cnt_loaded chain chain_act tables_ready
            x_loaded0 x_loaded1 stored0 stored1 blocks_final att_loaded0 att_loaded1
            td_done td_copied gates_done sig_r sig_z t_u tanh_d y_ready to_done out_done
            means_ready xc_ready ec_ready squares var_ready sd_ready xn_done norm_done h_kept xd_kept
            vt_done vt_copied qk_done qk_evac scan_done st_done ms_read v_ready std_ready
            t2_done t2_copied o_done od_done t3_done t3_copied g_done sig_g gru_u tanh_g mix_done res_done
            gathered0 gathered1 scattered0 scattered1 late_made late_saved late_loaded any_late park_loaded park_index park_done gather_index scatter_index count_seen""".split()
        q = {n: sem(n) for n in names}
        x_loaded, stored, att_loaded, gathered, scattered = (
            [q[n + "0"], q[n + "1"]] for n in ("x_loaded", "stored", "att_loaded", "gathered", "scattered"))

        def rows(t, start):
            return t[bass.ds(start, ROWS), :].rearrange("(p g) c -> p g c", p=P)

        loads = [
            (KR[:, :], key_r), (PR[:, :], prev_r), (AR_IN[:, :, :], attr_r), (KL[:, :], key_l), (NL[:, :], next_l),
            (KB, key_b), (GIDX[:, :], gidx), (EW[:, :], ew_l), (DH[:, :], deg_hist.partition_broadcast(P)),
            (WT2[:, 0, :], w_t), (WT2[:, 1, :], w_t),
            (WPRE[:, :, :], w_pre.rearrange("(a k) c -> k a c", k=C)), (WP0[:, :], w_post[0:C, :]),
            (WIH2[0:C, :], wih_t), (WIH2[C:P, :], wih_t), (WHH2[0:C, :], whh_t), (WHH2[C:P, :], whh_t),
            (WIHD[:, :, 0, :], wih_t.rearrange("k (g c) -> k g c", c=C)),
            (WIHD[:, :, 1, :], wih_t.rearrange("k (g c) -> k g c", c=C)),
            (WET[:, :], we_t), (WAU[AR - 1:AR, :], b_pre), (BPC[:, :], b_post),
            (BIC[0:C, :], bih_c), (BIC[C:P, :], bih_c), (BHC[0:C, :], bhh_c), (BHC[C:P, :], bhh_c),
            (BIR[:, :], bih_r), (BHR[:, :], bhh_r),
        ]
        for k in range(3):
            base = C + 4 * C * k
            cols = slice(C * k, C * k + C)
            loads += [(OW1[0:C, cols], w_post[base:base + C, :]), (OW1[C:P, cols], w_post[base + 3 * C:base + 4 * C, :]),
                      (OW2[0:C, cols], w_post[base + 2 * C:base + 3 * C, :]), (OW2[C:P, cols], w_post[base + C:base + 2 * C, :]),
                      (STDW[:, k, :], w_post[base + 3 * C:base + 4 * C, :])]
        SETUP_LOADS = 16 * len(loads)
        block = ctx.enter_context(nc.Block())

        def spread(ap, n):
            return ap.unsqueeze(len(ap.shape)).to_broadcast(list(ap.shape) + [n])

        E0 = GROUPS
        E1 = GROUPS + 2 * TILES

        @block.sync
        def _(sp):
            sp.dma_start(ID[:, :], ident).then_inc(q["ident_loaded"], 16)
            for to, of in loads:
                sp.dma_start(to, of).then_inc(q["setup_loaded"], 16)
            sp.dma_start(X[0][:, :, :], rows(x, 0)).then_inc(x_loaded[0], 16)
            sp.wait_ge(q["flags_made"], 1)
            sp.dma_start(keep_rows, KEEP[:, :]).then_inc(q["split_saved"], 16)
            sp.wait_ge(q["flags_made"], 2)
            sp.dma_start(attr_rows.rearrange("k p c -> p k c"), APART[:, :, :, :].rearrange("p i k c -> p (i k) c"))\
                .then_inc(q["split_saved"], 16)
            sp.wait_ge(q["flags_made"], 3)
            sp.dma_start(cnt_rows, CNT_R[:, :]).then_inc(q["cnt_saved"], 16)
            sp.wait_ge(q["cnt_saved"], 16)
            counts = cnt_rows.rearrange("p c -> (p c)").rearrange("(a t p) -> t a p", a=2, p=P)
            sp.dma_start(CNT_T[:, :, :], counts).then_inc(q["cnt_loaded"], 16)
            sp.wait_ge(q["late_made"], 1)
            sp.dma_start(late_cell, LATEI[:, :]).then_inc(q["late_saved"], 16)
            sp.wait_ge(q["late_saved"], 16)
            sp.dma_start(LATE[0:1, 0:BLOCKS], late_cell.rearrange("b a -> a b")).then_inc(q["late_loaded"], 16)
            sp.wait_ge(q["flags_made"], 4)
            sp.dma_start(wau_rows, WAUP[:, :, :]).then_inc(q["split_saved"], 16)
            sp.wait_ge(q["flags_made"], 5)
            sp.dma_start(bias_rows, BPART[:, :, :]).then_inc(q["split_saved"], 16)
            sp.wait_ge(q["split_saved"], 64)
            sp.wait_ge(q["zeroed"], 1)
            n = 0
            for j in range(PARTS):
                for i in range(PARTS):
                    at = (j * PARTS + i) * AR
                    sp.dma_start(WAUG[at:at + AR, 0:C], wau_rows[:, j, :]).then_inc(q["split_loaded"], 16)
                    n += 1
            for a in range(2):
                sp.dma_start(SBIAS[0:PARTS, a, :], bias_rows[0, :, :]).then_inc(q["split_loaded"], 16)
                n += 1
            assert n == 11

            keep_flat = keep_rows.rearrange("p c -> (p c)").rearrange("(a n) -> a n", a=1)
            attr_flat = attr_rows.rearrange("k p c -> k (p c)")

            def load_attributes(b):
                start = b.times(EB)
                start = start if isinstance(start, int) else sp.snap(start)
                wait(sp, q["qk_done"], b.next(-1).times(2))
                for j in range(PARTS):
                    sp.dma_start(ATT[b.par][j * PARTS * AR:(j + 1) * PARTS * AR, :], attr_flat[:, bass.ds(start, EB)])\
                        .then_inc(att_loaded[b.par], 16)
                sp.dma_start(ATT[b.par][KEEP_ROW:KEEP_ROW + 1, :], keep_flat[:, bass.ds(start, EB)])\
                    .then_inc(att_loaded[b.par], 16)

            load_attributes(At(None, 0))

            def step(i, more=True):
                here = i.times(STRIDE)
                here = here if isinstance(here, int) else sp.snap(here)
                if i.j is not None or i.off > 0:
                    sp.wait_ge(stored[1 - i.par], i.next(-1).pair(16))
                    sp.sem_inc(q["blocks_final"], 1)
                if more:
                    then = i.next().times(STRIDE)
                    then = then if isinstance(then, int) else sp.snap(then)
                    sp.dma_start(X[1 - i.par][:, :, :], rows(x, then)).then_inc(x_loaded[1 - i.par], 16)
                    load_attributes(i.next())
                sp.wait_ge(q["out_done"], i.times(CHUNKS, CHUNKS))
                sp.dma_start(rows(out, here), X[i.par][:, :, :]).then_inc(stored[i.par], 16)

            step(At(None, 0))
            step(At(None, 1))
            with sp.Fori(0, (BLOCKS - 3) // 2) as j:
                step(At(j, 2))
                step(At(j, 3))
            step(At(None, BLOCKS - 1), more=False)
            sp.wait_ge(stored[0], At(None, BLOCKS - 1).pair(16))
            sp.sem_inc(q["blocks_final"], 1)

        @block.gpsimd
        def _(pool):
            pool.memset(ATT[0][:, :], 0.0)
            pool.memset(ATT[1][:, :], 0.0)
            pool.memset(WAUG[:, :], 0.0)
            pool.memset(SBIAS[:, :, :], 0.0)
            pool.memset(ONESB[:, :], 1.0)
            pool.memset(SELK[:, :], 0.0)
            pool.memset(DW[:, :, :], 0.0)
            pool.memset(SW[:, :], 0.0)
            pool.memset(CARRY[:, :], 0.0)
            pool.memset(ONE[:, :], 1.0)
            pool.memset(ZERO1[:, :], 0.0).then_inc(q["zeroed"], 1)
            pool.wait_ge(q["zeroed"], 1)
            pool.affine_select(out=SELK[:, :], in_=SELK[:, :], compare_op=ALU.not_equal, fill=1.0, base=-KEEP_ROW,
                               pattern=[[0, P]], channel_multiplier=1)
            pool.iota(IDX[:, :], pattern=[[1, RC]], base=0, channel_multiplier=RC,
                      allow_small_or_imprecise_dtypes=True)
            pool.iota(LATEC[:, 1:2], pattern=[[1, 1]], base=2 * STRIDE, channel_multiplier=STRIDE,
                      allow_small_or_imprecise_dtypes=True).then_inc(q["iota_made"], 1)
            pool.wait_ge(q["setup_loaded"], SETUP_LOADS)
            pool.wait_ge(q["tables_ready"], 1)
            pool.wait_ge(q["any_late"], 1)

            bound = pool.to_reg(NODES - 1)
            any_late = pool.value_load(LATE[0:1, BLOCKS:BLOCKS + 1], min_val=0, max_val=1)

            def seen(sem, count):
                wait(pool, sem, count)
                pool.sem_inc(q["count_seen"], 1)

            def gather(b, part):
                if part == 0:
                    at = b.times(2 * TILES)
                    at = at if isinstance(at, int) else pool.snap(at)
                    pool.tensor_copy(IX[b.par][:, :], GIDX[:, bass.ds(at, 2 * TILES)]).then_inc(q["gather_index"], 1)
                    if b.j is not None or b.off > 1:
                        keep_x(b.next(-2))
                        seen(q["xd_kept"], b.times(1, -1))
                    seen(q["gather_index"], b.times(1, 1))
                for t in range(TH * part, TH * part + TH):
                    for w in range(2):
                        pool.indirect_dma_start(
                            XG[b.par][:, t, w, :], None, x,
                            bass.IndirectOffsetOnAxis(IX[b.par][:, 2 * t + w:2 * t + w + 1], 0),
                            bounds_check=bound, oob_is_err=False).then_inc(gathered[b.par], 16)

            def keep_x(b):
                pool.tensor_copy(XD[b.par][:, :, :], XG[b.par][:, :, 0, :]).then_inc(q["xd_kept"], 1)

            def centre_edges(b):
                seen(q["means_ready"], b.times(2, 1))
                wait_h = b.times(1)
                if not (isinstance(wait_h, int) and wait_h <= 0):
                    seen(q["h_kept"], wait_h)
                pool.tensor_tensor(EC[:, :, :, :].rearrange("p t w c -> p (t w) c"),
                                   XG[b.par][:, :, :, :].rearrange("p t w c -> p (t w) c"),
                                   spread(MEAN[:, E0:E1], C), ALU.subtract).then_inc(q["ec_ready"], 1)

            def centre_rows(b):
                seen(q["means_ready"], b.times(2, 2))
                wait_td = b.next(-1).times(CHUNKS)
                if not (isinstance(wait_td, int) and wait_td <= 0):
                    seen(q["td_done"], wait_td)
                pool.tensor_tensor(XN[b.par][:, :, :], X[b.par][:, :, :], spread(MEAN[:, 0:E0], C), ALU.subtract)\
                    .then_inc(q["xc_ready"], 1)

            def finish(b):
                if b.j is not None or b.off > 1:
                    seen(scattered[b.par], b.next(-2).pair(16 * TILES))
                seen(q["xd_kept"], b.times(1, 1))
                seen(q["mix_done"], b.times(1, 1))
                pool.tensor_tensor(RES[b.par][:, :, :], DG[:, :, :], XD[b.par][:, :, :], ALU.add)\
                    .then_inc(q["res_done"], 1)

            def scatter(b, last=False):
                at = b.times(TILES)
                at = at if isinstance(at, int) else pool.snap(at)
                pool.tensor_copy(SIX[b.par][:, :], SIDX[:, bass.ds(at, TILES)]).then_inc(q["scatter_index"], 1)
                seen(q["res_done"], b.times(1, 1))
                seen(q["scatter_index"], b.times(1, 1))
                seen(q["blocks_final"], BLOCKS if last else b.times(1, 2))
                send(b)

            def rows_to_out(index, results, done):
                for t in range(TILES):
                    pool.indirect_dma_start(
                        out, bass.IndirectOffsetOnAxis(index[:, t:t + 1], 0), results[:, t, :], None,
                        bounds_check=bound, oob_is_err=False).then_inc(done, 16)

            def send(b):
                number = b.times(1)
                number = number if isinstance(number, int) else pool.snap(number)
                with pool.If(any_late > 0):
                    for t in range(TILES):
                        pool.dma_start(parked[bass.ds(number, 1), :, C * t:C * t + C].rearrange("a p c -> p (a c)"),
                                       RES[b.par][:, t, :]).then_inc(scattered[b.par], 16)
                with pool.Else():
                    rows_to_out(SIX[b.par], RES[b.par], scattered[b.par])

            def step(i, rows=True, more=True, ends=True):
                if ends:
                    finish(i.next(-2))
                    scatter(i.next(-2))
                if more:
                    gather(i.next(2), 0)
                else:
                    keep_x(i)
                if rows:
                    centre_edges(i.next())
                    centre_rows(i.next())
                if more:
                    gather(i.next(2), 1)

            for b in range(2):
                for part in range(2):
                    gather(At(None, b), part)
                if b == 0:
                    centre_edges(At(None, 0))
                    centre_rows(At(None, 0))
            step(At(None, 0), ends=False)
            step(At(None, 1), ends=False)
            with pool.Fori(0, (BLOCKS - 5) // 2) as j:
                step(At(j, 2))
                step(At(j, 3))
            step(At(None, BLOCKS - 3))
            step(At(None, BLOCKS - 2), more=False)
            finish(At(None, BLOCKS - 3))
            finish(At(None, BLOCKS - 2))
            for b in range(BLOCKS - 3, BLOCKS):
                if b == BLOCKS - 1:
                    keep_x(At(None, b))
                    finish(At(None, b))
                scatter(At(None, b), last=True)
            for par in range(2):
                pool.wait_ge(scattered[par], 16 * TILES * ((BLOCKS + 1 - par) // 2))
            with pool.If(any_late > 0):
                with pool.Fori(0, BLOCKS) as b:
                    at = pool.snap(b * TILES)
                    pool.tensor_copy(SIX[0][:, :], SIDX[:, bass.ds(at, TILES)]).then_inc(q["park_index"], 1)
                    pool.dma_start(RES[0][:, :, :].rearrange("p t c -> p (t c)"),
                                   parked[bass.ds(b, 1), :, :].rearrange("a p c -> p (a c)")).then_inc(q["park_loaded"], 16)
                    pool.wait_ge(q["park_index"], b + 1)
                    pool.sem_inc(q["count_seen"], 1)
                    pool.wait_ge(q["park_loaded"], b * 16 + 16)
                    pool.sem_inc(q["count_seen"], 1)
                    rows_to_out(SIX[0], RES[0], q["park_done"])
                    pool.wait_ge(q["park_done"], b * (16 * TILES) + 16 * TILES)
                    pool.sem_inc(q["count_seen"], 1)
            with pool.Else():
                pool.nop()

        @block.vector
        def _(dve):
            done = [0]
            base = [At(None, 0), 0]

            def chained(ins):
                ins.then_inc(q["chain"], 1)
                done[0] += 1

            def settle():
                dve.wait_ge(q["chain"], base[0].times(PER_STEP, base[1] + done[0]))

            def link(ins):
                chained(ins)
                settle()

            tt, ts, stt, copy = dve.tensor_tensor, dve.tensor_scalar, dve.scalar_tensor_tensor, dve.tensor_copy

            dve.wait_ge(q["setup_loaded"], SETUP_LOADS)
            dve.wait_ge(q["iota_made"], 1)
            copy(W2[:, :], KR[:, :])
            link(copy(LOC[:, :], PR[:, :]))
            link(tt(W2[:, :], W2[:, :], LOC[:, :], ALU.is_equal))
            copy(KEEP[:, :], W2[:, :]).then_inc(q["flags_made"], 1)
            ew_r = AR_IN[:, 3, :]
            for k in range(3):
                tt(AE[:, k, :], AR_IN[:, k, :], ew_r, ALU.mult)
            copy(AE[:, 3, :], ew_r)
            link(dve.memset(AE[:, 4, :], 1.0))
            for i in range(PARTS):
                link(copy(APART[:, i, :, :], AE[:, :, :]))
                if i < PARTS - 1:
                    link(tt(AE[:, :, :], AE[:, :, :], APART[:, i, :, :], ALU.subtract))
            dve.sem_inc(q["flags_made"], 1)
            link(tt(W2[:, :], W2[:, :], IDX[:, :], ALU.mult))
            link(tt(W2[:, :], IDX[:, :], W2[:, :], ALU.subtract))
            link(dve.tensor_tensor_scan(LOC[:, :], W2[:, :], W2[:, :], 0.0, ALU.max, ALU.max))
            copy(LAST[:, :], LOC[:, RC - 1:RC]).then_inc(q["prep_ready"], 1)
            dve.wait_ge(q["prep"], 1)
            link(copy(LG[0:1, 0:P], GATE[0:1, 0, 0:P]))
            link(dve.tensor_tensor_scan(CARRY[:, 1:P + 1], LG[0:1, 0:P], LG[0:1, 0:P], 0.0, ALU.max, ALU.max))
            dve.sem_inc(q["prep_ready"], 1)
            dve.wait_ge(q["prep"], 2)
            link(copy(LAST[:, :], TIN[:, 0:1]))
            link(stt(W2[:, :], LOC[:, :], LAST[:, 0:1], IDX[:, :], ALU.max, ALU.subtract))
            ts(CNT_R[:, :], W2[:, :], -1.0, 1.0, ALU.mult, ALU.add).then_inc(q["flags_made"], 1)
            copy(W0[:, :], KL[:, :])
            link(copy(W1[:, :], NL[:, :]))
            link(tt(W1[:, :], W0[:, :], W1[:, :], ALU.is_equal))
            link(stt(W1[:, :], W1[:, :], float(OUT_OF_RANGE), W0[:, :], ALU.mult, ALU.add))
            link(copy(SIDX[:, :], W1[:, :]))

            link(copy(KBF, KB))
            link(dve.tensor_reduce(LATEC[:, 0:1], KBF, AX, ALU.max))
            link(tt(LATEC[:, 2:3], LATEC[:, 0:1], LATEC[:, 1:2], ALU.is_ge))
            copy(LATEI[:, :], LATEC[:, 2:3]).then_inc(q["late_made"], 1)
            dve.wait_ge(q["late_loaded"], 16)
            dve.tensor_reduce(LATE[:, BLOCKS:BLOCKS + 1], LATE[:, 0:BLOCKS - 3], AX, ALU.max).then_inc(q["any_late"], 1)

            dve.wait_ge(q["prep"], 3)
            copy(QW[0:C, 0:C], GATE[0:C, 1, 0:C])
            ts(QW[0:C, C:P], GATE[0:C, 1, 0:C], -1.0, None, ALU.mult)
            copy(QW[C:P, 0:C], GATE[C:P, 1, C:P])
            ts(QW[C:P, C:P], GATE[C:P, 1, C:P], -1.0, None, ALU.mult)
            copy(M1D[:, 0, :], GATE[0:C, 2, 0:C])
            copy(M1D[:, 1, :], GATE[0:C, 2, 0:C])
            copy(WAU[0:4, :], GATE[0:4, 3, 0:C])
            ts(OW2[C:P, :], OW2[C:P, :], -1.0, None, ALU.mult)
            tt(BIC[:, 0:2], BIC[:, 0:2], BHC[:, 0:2], ALU.add)
            tt(BROW[:, 0:2 * C], BIR[:, 0:2 * C], BHR[:, 0:2 * C], ALU.add)
            copy(BROW[:, 2 * C:3 * C], BHR[:, 2 * C:3 * C])
            link(copy(BROW[:, 3 * C:4 * C], BIR[:, 2 * C:3 * C]))
            tt(BROW[:, 0:2 * C], BROW[:, 0:2 * C], EP[0:1, 0:2 * C], ALU.add)
            tt(BROW[:, 3 * C:4 * C], BROW[:, 3 * C:4 * C], EP[0:1, 2 * C:3 * C], ALU.add)
            dve.wait_ge(q["logs_ready"], 1)
            link(dve.tensor_reduce(AVG[:, :], LDH[:, :], AX, ALU.add))
            link(ts(AVG[:, :], AVG[:, :], 1.0 / 11, None, ALU.mult))
            dve.reciprocal(IAVG[:, :], AVG[:, :])
            link(dve.reciprocal(NOEDGE[:, 4:5], NOEDGE[:, 3:4]))
            tt(NOEDGE[:, 1:2], NOEDGE[:, 3:4], IAVG[:, :], ALU.mult)
            link(tt(NOEDGE[:, 2:3], NOEDGE[:, 4:5], AVG[:, :], ALU.mult))
            link(tt(NOEDGE[:, 2:3], NOEDGE[:, 2:3], NOEDGE[:, 1:2], ALU.mult))
            link(ts(NOEDGE[:, 1:3], NOEDGE[:, 1:3], EPS ** 0.5, None, ALU.mult))
            link(dve.memset(NOEDGE[:, 0:1], EPS ** 0.5))
            dve.sem_inc(q["prep_ready"], 1)
            for i in range(PARTS):
                link(copy(WAUP[:, i, :], WAU[:, :] if i == 0 else WAUR[:, :]))
                if i < PARTS - 1:
                    link(tt(WAUR[:, :], WAU[:, :] if i == 0 else WAUR[:, :], WAUP[:, i, :], ALU.subtract))
            dve.sem_inc(q["flags_made"], 1)
            for i in range(PARTS):
                link(copy(BPART[:, i, :], BROW[:, :] if i == 0 else BRES[:, :]))
                if i < PARTS - 1:
                    link(tt(BRES[:, :], BROW[:, :] if i == 0 else BRES[:, :], BPART[:, i, :], ALU.subtract))
            dve.sem_inc(q["flags_made"], 1)
            dve.wait_ge(q["prep"], 4)
            link(tt(BV[:, :], TOUT[0:C, 0:1], BPC[:, :], ALU.add))
            dve.sem_inc(q["prep_ready"], 1)
            for g in range(2):
                for h in range(2):
                    r = slice(C * h, C * h + C)
                    tt(DW[r, g, r], TIN[r, C * g:C * g + C], WHH2[r, C * g:C * g + C], ALU.add)
                copy(SW[C:P, C * g:C * g + C], WIH2[C:P, C * g:C * g + C])
                tt(SW[0:C, C * g:C * g + C], TIN[0:C, C * g:C * g + C], WHH2[0:C, C * g:C * g + C], ALU.add)
            for h in range(2):
                r = slice(C * h, C * h + C)
                copy(DW[r, 2, r], WHH2[r, 2 * C:3 * C])
                copy(DW[r, 3, r], TIN[r, 2 * C:3 * C])
            copy(SW[0:C, 2 * C:3 * C], WHH2[0:C, 2 * C:3 * C])
            copy(SW[0:C, 3 * C:4 * C], TIN[0:C, 2 * C:3 * C])
            link(copy(SW[C:P, 3 * C:4 * C], WIH2[C:P, 2 * C:3 * C]))
            dve.wait_ge(q["prep"], 5)
            tt(DB[:, 0:2], EP[:, 0:2], BIC[:, 0:2], ALU.add)
            copy(DB[:, 2:3], BHC[:, 2:3])
            link(tt(DB[:, 3:4], EP[:, 2:3], BIC[:, 2:3], ALU.add))
            dve.wait_ge(q["split_loaded"], 16 * 11)
            link(copy(WAUG[:, C:P], WAUG[:, 0:C]))
            link(ts(WAUG[:, C:P], WAUG[:, 0:C], -1.0, None, ALU.mult))
            dve.wait_ge(q["prep"], 6)
            copy(W0[:, 0:RC // 2], GATE[:, 0, 0:RC // 2])
            link(copy(W0[:, RC // 2:RC], GATE[:, 0, P:P + RC // 2]))
            dve.sem_inc(q["prep_ready"], 1)
            copy(COEFS[:, :, 3], EW[:, :])
            dve.reciprocal(COEFS[:, :, 0], W0[:, :])
            dve.wait_ge(q["logs_ready"], 2)
            dve.reciprocal(ILG[:, :], LG[:, :])
            link(ts(COEFS[:, :, 1], LG[:, :], IAVG[:, 0:1], None, ALU.mult))
            link(ts(ILG[:, :], ILG[:, :], AVG[:, 0:1], None, ALU.mult))
            link(tt(COEFS[:, :, 2], ILG[:, :], COEFS[:, :, 1], ALU.mult))
            dve.sem_inc(q["tables_ready"], 1)

            def edge_means(b):
                dve.wait_ge(gathered[b.par], b.pair(16 * 2 * TILES))
                xg = XG[b.par][:, :, :, :].rearrange("p t w c -> p (t w) c")
                link(dve.tensor_reduce(SUM[:, E0:E1], xg, AX, ALU.add))
                ts(MEAN[:, E0:E1], SUM[:, E0:E1], 1.0 / C, None, ALU.mult).then_inc(q["means_ready"], 1)

            def row_means(b):
                dve.wait_ge(x_loaded[b.par], b.pair(16))
                link(dve.tensor_reduce(SUM[:, 0:E0], X[b.par][:, :, :], AX, ALU.add))
                ts(MEAN[:, 0:E0], SUM[:, 0:E0], 1.0 / C, None, ALU.mult).then_inc(q["means_ready"], 1)

            def variance(b):
                dve.wait_ge(q["squares"], b.times(2, 1))
                dve.tensor_reduce(SSQ[:, E0:E1], ESQ[:, :, :], AX, ALU.add)
                dve.wait_ge(q["squares"], b.times(2, 2))
                link(dve.tensor_reduce(SSQ[:, 0:E0], SQ[:, :, :], AX, ALU.add))
                wait(dve, q["xn_done"], b.times(1))
                ts(VAR[:, :], SSQ[:, :], 1.0 / C, EPS, ALU.mult, ALU.add).then_inc(q["var_ready"], 1)

            def normalise(b):
                dve.wait_ge(q["sd_ready"], b.times(1, 1))
                link(dve.reciprocal(RSTD[:, :], VAR[:, :]))
                tt(XN[b.par][:, :, :], XN[b.par][:, :, :], spread(RSTD[:, 0:E0], C), ALU.mult).then_inc(q["xn_done"], 1)

            def weighted(b):
                at = b.times(TILES)
                at = at if isinstance(at, int) else dve.snap(at)
                link(ts(COEF[b.par][:, :, :], COEFS[:, bass.ds(at, TILES), :], 1.0, None, ALU.mult))
                rs = RSTD[:, E0:E1].rearrange("p (t w) -> p t w", w=2)
                link(tt(RW[:, :, :], rs, spread(COEF[b.par][:, :, 3], 2), ALU.mult))
                wait(dve, q["vt_done"], b.times(1))
                stt(V[:, :, :].rearrange("p t (w c) -> p t w c", w=2), EC[:, :, :, :], 0.0, spread(RW[:, :, :], C),
                    ALU.max, ALU.mult).then_inc(q["norm_done"], 1)

            def keep_h(b):
                stt(HO[b.par][:, :, 0:C], EC[:, :, 0, :], 0.0,
                    spread(RSTD[:, E0:E1].rearrange("p (t w) -> p t w", w=2)[:, :, 0], C), ALU.max, ALU.mult)\
                    .then_inc(q["h_kept"], 1)

            def gate_n(i, c):
                dve.wait_ge(q["sig_r"], i.times(CHUNKS, c + 1))
                dve.wait_ge(q["gates_done"], i.times(4 * CHUNKS, 4 * c + 3))
                link(stt(T[:, :], GATE[:, 2, :], DB[:, 2:3], SR[c % 2][:, :], ALU.add, ALU.mult))
                dve.wait_ge(q["gates_done"], i.times(4 * CHUNKS, 4 * c + 4))
                wait(dve, q["tanh_d"], i.times(CHUNKS, c - 1))
                tt(U[c % 2][:, :], T[:, :], GATE[:, 3, :], ALU.add).then_inc(q["t_u"], 1)

            def mix(i, c):
                dve.wait_ge(q["tanh_d"], i.times(CHUNKS, c + 1))
                link(tt(D[:, :], HT[c % 2][:, :], NN[c % 2][:, :], ALU.subtract))
                dve.wait_ge(q["sig_z"], i.times(CHUNKS, c + 1))
                link(tt(D[:, :], D[:, :], SZ[c % 2][:, :], ALU.mult))
                wait(dve, q["to_done"], i.times(CHUNKS, c - 1))
                tt(Y[c % 2][:, :], D[:, :], NN[c % 2][:, :], ALU.add).then_inc(q["y_ready"], 1)

            def add_x(i, c):
                dve.wait_ge(q["to_done"], i.times(CHUNKS, c + 1))
                xs = X[i.par][:, GC * c:GC * c + GC, :].rearrange("p g c -> p (g c)")
                tt(xs, xs, TOUT[:, :], ALU.add).then_inc(q["out_done"], 1)

            def scan(i, h):
                cols = slice(HALF * h, HALF * h + HALF)
                dve.wait_ge(q["qk_evac"], i.times(2, h + 1))
                wait(dve, q["st_done"], i.times(1))
                wait(dve, q["o_done"], i.next(-1).times(2))
                first = h == 0 and i.j is None and i.off == 0
                before = EB - 1 if h == 0 else HALF - 1
                s0 = 0.0 if first else S[:, before:before + 1]
                m0 = -BIG if first else MX[i.par if h else 1 - i.par][:, before:before + 1]
                dve.tensor_tensor_scan(S[:, cols], EP[:, HALF:EB], H[:, :], s0, ALU.mult, ALU.add)
                dve.tensor_tensor_scan(MX[i.par][:, cols], CAP[:, :], EP[:, 0:HALF], m0, ALU.min, ALU.max)\
                    .then_inc(q["scan_done"], 1)

            def moments(i):
                dve.wait_ge(q["st_done"], i.times(1, 1))
                wait(dve, q["t2_done"], i.times(1))
                tt(MS[:, :, :], EPT, spread(COEF[i.par][:, :, 0], P), ALU.mult).then_inc(q["ms_read"], 1)
                dve.wait_ge(q["ms_read"], i.times(1, 1))
                link(tt(M2[:, :, :], MS[:, :, 0:C], MS[:, :, 0:C], ALU.mult))
                link(tt(MS[:, :, C:P], MS[:, :, C:P], M2[:, :, :], ALU.subtract))
                ts(MS[:, :, C:P], MS[:, :, C:P], 0.0, EPS, ALU.max, ALU.add).then_inc(q["v_ready"], 1)

            def post(b, h):
                tiles = slice(TH * h, TH * h + TH)
                dve.wait_ge(q["o_done"], b.times(2, h + 1))
                t1 = T1[:, :, :].rearrange("p t (k c) -> p t k c", k=2)
                scalers = spread(COEF[b.par][:, tiles, 1:3], C)
                link(tt(t1, EPW[:, :, C:3 * C].rearrange("p t (k c) -> p t k c", k=2), scalers, ALU.mult))
                link(tt(OS[:, :, :], T1[:, :, 0:C], T1[:, :, C:P], ALU.add))
                tt(HO[b.par][:, tiles, C:P], OS[:, :, :], EPW[:, :, 0:C], ALU.add).then_inc(q["od_done"], 1)

            def edge_gate_n(b, h):
                tiles = slice(TH * h, TH * h + TH)
                dve.wait_ge(q["sig_g"], b.times(2, h + 1))
                link(tt(TG[:, :, :], EPW[:, :, 2 * C:3 * C], RZ[:, tiles, 0:C], ALU.mult))
                tt(UG[:, tiles, :], TG[:, :, :], EPW[:, :, 3 * C:4 * C], ALU.add).then_inc(q["gru_u"], 1)

            def edge_mix(b):
                dve.wait_ge(q["tanh_g"], b.times(2, 2))
                wait(dve, q["res_done"], b.times(1))
                link(tt(DG[:, :, :], HO[b.par][:, :, 0:C], NG[:, :, :], ALU.subtract))
                link(tt(DG[:, :, :], DG[:, :, :], RZ[:, :, C:P], ALU.mult))
                tt(DG[:, :, :], DG[:, :, :], NG[:, :, :], ALU.add).then_inc(q["mix_done"], 1)

            def step(i, new=True, old=True):
                p = i.next(-1)
                done[0] = 0
                gate_n(i, 0)
                scan(i, 0)
                mix(i, 0)
                if new:
                    edge_means(i.next())
                if old:
                    post(p, 0)
                gate_n(i, 1)
                add_x(i, 0)
                scan(i, 1)
                if new:
                    row_means(i.next())
                mix(i, 1)
                if old:
                    post(p, 1)
                gate_n(i, 2)
                add_x(i, 1)
                moments(i)
                mix(i, 2)
                gate_n(i, 3)
                add_x(i, 2)
                if old:
                    edge_gate_n(p, 0)
                if new:
                    variance(i.next())
                if old:
                    edge_gate_n(p, 1)
                mix(i, 3)
                if new:
                    normalise(i.next())
                    weighted(i.next())
                add_x(i, 3)
                if old:
                    edge_mix(p)
                if new:
                    keep_h(i.next())

            edge_means(At(None, 0))
            row_means(At(None, 0))
            variance(At(None, 0))
            normalise(At(None, 0))
            weighted(At(None, 0))
            keep_h(At(None, 0))
            base[1] = done[0]
            step(At(None, 0), old=False)
            at_one = base[1] + done[0]
            base[:] = [At(None, 1), at_one - PER_STEP]
            step(At(None, 1))
            assert done[0] == PER_STEP, done[0]
            with dve.Fori(0, (BLOCKS - 3) // 2) as j:
                for k in range(2):
                    base[0] = At(j, 2 + k)
                    step(At(j, 2 + k))
            base[0] = At(None, BLOCKS - 1)
            step(At(None, BLOCKS - 1), new=False)
            last = At(None, BLOCKS - 1)
            post(last, 0)
            post(last, 1)
            edge_gate_n(last, 0)
            edge_gate_n(last, 1)
            edge_mix(last)

        @block.scalar
        def _(act):
            def act_on(out_, in_, func, **kw):
                return act.activation(out_, in_, func, **kw)

            act.wait_ge(q["setup_loaded"], SETUP_LOADS)
            act.wait_ge(q["zeroed"], 1)
            act_on(LDH[:, :], DH[:, :], ACT.Ln, bias=ONE[:, 0:1])
            act_on(NOEDGE[:, 3:4], ONE[:, :], ACT.Ln, bias=ONE[:, 0:1]).then_inc(q["logs_ready"], 1)
            act.wait_ge(q["prep_ready"], 5)
            act_on(LG[:, :], W0[:, :], ACT.Ln, bias=ONE[:, 0:1]).then_inc(q["logs_ready"], 1)

            def squares(b):
                act.wait_ge(q["ec_ready"], b.times(1, 1))
                wait(act, q["var_ready"], b.times(1))
                act_on(ESQ[:, :, :], EC[:, :, :, :].rearrange("p t w c -> p (t w) c"), ACT.Square)\
                    .then_inc(q["squares"], 1)
                act.wait_ge(q["xc_ready"], b.times(1, 1))
                act_on(SQ[:, :, :], XN[b.par][:, :, :], ACT.Square).then_inc(q["squares"], 1)

            def roots(i, new=True, cur=True):
                if cur:
                    act.wait_ge(q["v_ready"], i.times(1, 1))
                    act_on(MS[:, :, C:P], MS[:, :, C:P], ACT.Sqrt).then_inc(q["std_ready"], 1)
                if new:
                    b = i.next()
                    act.wait_ge(q["var_ready"], b.times(1, 1))
                    act_on(VAR[:, :], VAR[:, :], ACT.Sqrt).then_inc(q["sd_ready"], 1)

            def take_h(i, c):
                act.wait_ge(q["td_done"], i.times(CHUNKS, c + 1))
                wait(act, q["gates_done"], i.times(4 * CHUNKS, 4 * (c - 1)))
                wait(act, q["y_ready"], i.times(CHUNKS, c - 1))
                act_on(HT[c % 2][:, :], TIN[:, :], ACT.Relu).then_inc(q["td_copied"], 1)

            def gates_rz(i, c):
                act.wait_ge(q["gates_done"], i.times(4 * CHUNKS, 4 * c + 1))
                wait(act, q["t_u"], i.times(CHUNKS, c - 1))
                act_on(SR[c % 2][:, :], GATE[:, 0, :], ACT.Sigmoid, bias=DB[:, 0:1]).then_inc(q["sig_r"], 1)
                act.wait_ge(q["gates_done"], i.times(4 * CHUNKS, 4 * c + 2))
                wait(act, q["y_ready"], i.times(CHUNKS, c - 1))
                act_on(SZ[c % 2][:, :], GATE[:, 1, :], ACT.Sigmoid, bias=DB[:, 1:2]).then_inc(q["sig_z"], 1)

            def gate_n(i, c):
                act.wait_ge(q["t_u"], i.times(CHUNKS, c + 1))
                wait(act, q["y_ready"], i.times(CHUNKS, c - 1))
                act_on(NN[c % 2][:, :], U[c % 2][:, :], ACT.Tanh, bias=DB[:, 3:4]).then_inc(q["tanh_d"], 1)

            def messages(i, h):
                act.wait_ge(q["qk_done"], i.times(2, h + 1))
                wait(act, q["scan_done"], i.times(2, h))
                act_on(H[0:C, :], EP[0:C, 0:HALF], ACT.Copy)
                act_on(H[C:P, :], EP[C:P, 0:HALF], ACT.Square)
                act_on(CAP[:, :], EP[:, HALF:EB], ACT.Copy, scale=2 * BIG, bias=-BIG).then_inc(q["qk_evac"], 1)

            def edge_gates_rz(b, h):
                tiles = slice(TH * h, TH * h + TH)
                act.wait_ge(q["g_done"], b.times(2, h + 1))
                wait(act, q["mix_done"], b.times(1))
                act_on(RZ[:, tiles, :], EPW[:, :, 0:2 * C], ACT.Sigmoid).then_inc(q["sig_g"], 1)

            def edge_gate_n(b, h):
                tiles = slice(TH * h, TH * h + TH)
                act.wait_ge(q["gru_u"], b.times(2, h + 1))
                act_on(NG[:, tiles, :], UG[:, tiles, :], ACT.Tanh).then_inc(q["tanh_g"], 1)

            def take_v(i):
                act.wait_ge(q["vt_done"], i.times(1, 1))
                wait(act, q["qk_done"], i.times(2))
                act_on(VTS[:, :], EP[:, :], ACT.Copy).then_inc(q["vt_copied"], 1)

            def take_moments(b):
                act.wait_ge(q["t2_done"], b.times(1, 1))
                wait(act, q["o_done"], b.times(2))
                act_on(MST[:, :], EP[:, :], ACT.Copy).then_inc(q["t2_copied"], 1)

            def take_ho(b):
                act.wait_ge(q["t3_done"], b.times(1, 1))
                wait(act, q["g_done"], b.times(2))
                act_on(HOT[:, :], EP[:, :], ACT.Copy).then_inc(q["t3_copied"], 1)

            def start(i):
                take_h(i, 0)
                take_v(i)
                gates_rz(i, 0)

            def step(i, new=True, old=True):
                p = i.next(-1)
                take_h(i, 1)
                messages(i, 0)
                gate_n(i, 0)
                gates_rz(i, 1)
                take_h(i, 2)
                messages(i, 1)
                gate_n(i, 1)
                gates_rz(i, 2)
                take_h(i, 3)
                gate_n(i, 2)
                if new:
                    squares(i.next())
                gates_rz(i, 3)
                if old:
                    take_ho(p)
                gate_n(i, 3)
                if old:
                    edge_gates_rz(p, 0)
                    edge_gate_n(p, 0)
                    edge_gates_rz(p, 1)
                    edge_gate_n(p, 1)
                roots(i, new)
                take_moments(i)
                if new:
                    start(i.next())

            squares(At(None, 0))
            roots(At(None, -1), cur=False)
            start(At(None, 0))
            step(At(None, 0), old=False)
            step(At(None, 1))
            with act.Fori(0, (BLOCKS - 3) // 2) as j:
                step(At(j, 2))
                step(At(j, 3))
            last = At(None, BLOCKS - 1)
            step(last, new=False)
            take_ho(last)
            for h in range(2):
                edge_gates_rz(last, h)
                edge_gate_n(last, h)

        @block.tensor
        def _(pe):
            mm, tr = pe.matmul, pe.transpose
            pe.wait_ge(q["ident_loaded"], 16)
            pe.wait_ge(q["setup_loaded"], SETUP_LOADS)
            pe.wait_ge(q["prep_ready"], 1)
            mm(GATE[0:1, 0, 0:P], LAST[:, :], ID[:, :], start=True, stop=True).then_inc(q["prep"], 1)
            pe.wait_ge(q["zeroed"], 1)
            pe.wait_ge(q["prep_ready"], 2)
            mm(TIN[:, 0:1], CARRY[0:1, 0:P], ONE[0:1, 0:1], start=True, stop=True).then_inc(q["prep"], 1)
            mm(GATE[:, 1, 0:P], WT2[:, :, :].rearrange("k a c -> k (a c)"),
               WPRE[:, 0:2, :].rearrange("k a c -> k (a c)"), start=True, stop=True)
            mm(GATE[0:C, 2, 0:C], WP0[:, :], WT2[:, 0, :], start=True, stop=True)
            mm(GATE[0:4, 3, 0:C], WET[:, :], WPRE[:, 2, :], start=True, stop=True)
            mm(EP[0:1, 0:3 * C], BPC[:, :], WIH2[0:C, :], start=True, stop=True).then_inc(q["prep"], 1)
            pe.wait_ge(q["prep_ready"], 3)
            mm(TIN[:, 0:3 * C], M1D[:, :, :].rearrange("k a c -> k (a c)"), WIH2[0:C, :], start=True, stop=True)
            for k in range(3):
                last = mm(TOUT[0:C, 0:1], STDW[:, k, :], NOEDGE[0:C, k:k + 1], start=k == 0, stop=k == 2)
            last.then_inc(q["prep"], 1)
            pe.wait_ge(q["prep_ready"], 4)
            for g in range(3):
                last = mm(EP[:, g:g + 1], WIHD[:, g, :, :].rearrange("k a c -> k (a c)"), BV[:, :], start=True, stop=True)
            last.then_inc(q["prep"], 1)
            pe.wait_ge(q["cnt_loaded"], 16)
            half = RC // 2
            tr(GATE[:, 0, 0:half], CNT_T[:, 0, :], ID[0:half, 0:half])
            tr(GATE[:, 0, P:P + half], CNT_T[:, 1, :], ID[0:half, 0:half]).then_inc(q["prep"], 1)
            pe.wait_ge(q["tables_ready"], 1)

            def rows_in(i, c):
                pe.wait_ge(q["xn_done"], i.times(1, 1))
                wait(pe, q["td_copied"], i.times(CHUNKS, c))
                for k in range(4):
                    g = GC * c + 2 * k
                    last = tr(TIN[:, P * k:P * k + P], XN[i.par][:, g:g + 2, :].rearrange("p g c -> p (g c)"), ID[:, :])
                last.then_inc(q["td_done"], 1)

            def gates(i, c):
                pe.wait_ge(q["td_copied"], i.times(CHUNKS, c + 1))
                for g, free in enumerate((q["sig_r"], q["sig_z"], q["t_u"], q["t_u"])):
                    wait(pe, free, i.times(CHUNKS, c))
                    mm(GATE[:, g, :], DW[:, g, :], HT[c % 2][:, :], start=True, stop=True).then_inc(q["gates_done"], 1)

            def rows_out(i, c):
                pe.wait_ge(q["y_ready"], i.times(CHUNKS, c + 1))
                wait(pe, q["out_done"], i.times(CHUNKS, c))
                for k in range(4):
                    last = tr(TOUT[:, P * k:P * k + P], Y[c % 2][:, P * k:P * k + P], ID[:, :])
                last.then_inc(q["to_done"], 1)

            def tiles_turned(of, done_):
                for t in range(TILES):
                    last = tr(EPT[:, t, :], of[:, t, :], ID[:, :])
                last.then_inc(done_, 1)

            def turn_moments(i):
                wait(pe, q["gru_u"], i.times(2))
                pe.wait_ge(q["std_ready"], i.times(1, 1))
                tiles_turned(MS, q["t2_done"])

            def turn_v(i):
                pe.wait_ge(q["norm_done"], i.times(1, 1))
                wait(pe, q["t2_copied"], i.times(1))
                tiles_turned(V, q["vt_done"])

            def messages(i, h):
                if h == 0:
                    pe.wait_ge(q["vt_copied"], i.times(1, 1))
                    pe.wait_ge(att_loaded[i.par], i.pair(16 * (PARTS + 1)))
                else:
                    wait(pe, q["od_done"], i.next(-1).times(2, 1))
                    pe.wait_ge(q["scan_done"], i.times(2, 1))
                cols = slice(HALF * h, HALF * h + HALF)
                att = ATT[i.par][:, cols]
                mm(EP[:, 0:HALF], QW[:, :], VTS[:, cols], start=True, stop=False)
                mm(EP[:, 0:HALF], WAUG[:, :], att, start=False, stop=True)
                mm(EP[:, HALF:EB], SELK[:, :], att, start=True, stop=True).then_inc(q["qk_done"], 1)

            def post(b, h, scans):
                pe.wait_ge(q["t2_copied"], b.times(1, 1))
                if scans is not None:
                    pe.wait_ge(q["scan_done"], scans.times(2, h + 1))
                elif h:
                    pe.wait_ge(q["od_done"], b.times(2, 1))
                for t in range(TH):
                    cols = slice(HALF * h + P * t, HALF * h + P * t + P)
                    mm(EPW[:, t, 0:3 * C], MST[:, cols], OW1[:, :], start=True, stop=False)
                    last = mm(EPW[:, t, 0:3 * C], MX[b.par][:, cols], OW2[:, :], start=False, stop=True)
                last.then_inc(q["o_done"], 1)

            def turn_sums(i):
                wait(pe, q["od_done"], i.times(2))
                pe.wait_ge(q["scan_done"], i.times(2, 2))
                for t in range(TILES):
                    last = tr(EPT[:, t, :], S[:, P * t:P * t + P], ID[:, :])
                last.then_inc(q["st_done"], 1)

            def turn_ho(b, sums):
                if sums is not None:
                    pe.wait_ge(q["ms_read"], sums.times(1, 1))
                pe.wait_ge(q["h_kept"], b.times(1, 1))
                pe.wait_ge(q["od_done"], b.times(2, 2))
                tiles_turned(HO[b.par], q["t3_done"])

            def edge_gates(b, h):
                pe.wait_ge(q["t3_copied"], b.times(1, 1))
                if h:
                    pe.wait_ge(q["gru_u"], b.times(2, 1))
                for a in range(2):
                    mm(EP[:, HALF * a:HALF * a + HALF], ONESB[:, :], SBIAS[:, :, :].rearrange("p a c -> p (a c)"),
                       start=True, stop=False, skip_group_check=True)
                    for t in (2 * a, 2 * a + 1):
                        cols = slice(HALF * h + P * t, HALF * h + P * t + P)
                        last = mm(EPW[:, t, :], HOT[:, cols], SW[:, :], start=False, stop=t % 2 == 1, skip_group_check=True)
                last.then_inc(q["g_done"], 1)

            def start(i):
                rows_in(i, 0)
                turn_v(i)
                gates(i, 0)

            def step(i, new=True, old=True):
                p = i.next(-1)
                rows_in(i, 1)
                messages(i, 0)
                gates(i, 1)
                rows_in(i, 2)
                if old:
                    post(p, 0, i)
                rows_out(i, 0)
                messages(i, 1)
                gates(i, 2)
                rows_in(i, 3)
                if old:
                    post(p, 1, i)
                rows_out(i, 1)
                turn_sums(i)
                gates(i, 3)
                if old:
                    turn_ho(p, i)
                    edge_gates(p, 0)
                rows_out(i, 2)
                if old:
                    edge_gates(p, 1)
                rows_out(i, 3)
                turn_moments(i)
                if new:
                    start(i.next())

            start(At(None, 0))
            step(At(None, 0), old=False)
            step(At(None, 1))
            with pe.Fori(0, (BLOCKS - 3) // 2) as j:
                step(At(j, 2))
                step(At(j, 3))
            last = At(None, BLOCKS - 1)
            step(last, new=False)
            post(last, 0, None)
            post(last, 1, None)
            turn_ho(last, None)
            edge_gates(last, 0)
            edge_gates(last, 1)


def kernel(x, src, dst, edge_attr_4, L0_gnn_deg_hist, L0_gnn_weight, L0_gnn_W_e, L0_gnn_b_e, L0_gnn_W_pre, L0_gnn_b_pre,
           L0_gnn_W_post, L0_gnn_b_post, L0_gnn_W_ih, L0_gnn_W_hh, L0_gnn_b_ih, L0_gnn_b_hh):
    import numpy as np
    import concourse.bacc as bacc
    from concourse.bass_utils import run_bass_kernel_spmd

    x, src, dst, attr = (np.asarray(a) for a in (x, src, dst, edge_attr_4))
    pad = EDGES_PADDED - EDGES

    def padded(a, value):
        return np.concatenate([a, np.full((pad,) + a.shape[1:], value, a.dtype)])

    def by_tile(a):
        return a.reshape(ALL_TILES, P).T

    key = padded(dst, NODES)
    ends = np.full(1, NODES, dst.dtype), np.full(1, -1, dst.dtype)
    gidx = np.stack([by_tile(padded(dst, 0)), by_tile(padded(src, 0))], axis=2).reshape(P, 2 * ALL_TILES)
    attr = padded(attr, 0)
    w_ih, w_hh = np.asarray(L0_gnn_W_ih), np.asarray(L0_gnn_W_hh)
    b_ih, b_hh = np.asarray(L0_gnn_b_ih), np.asarray(L0_gnn_b_hh)
    arrays = {
        "x": x, "gidx": gidx, "key_l": by_tile(key), "next_l": by_tile(np.concatenate([key[1:], ends[0]])),
        "key_r": key.reshape(P, RC), "prev_r": np.concatenate([ends[1], key[:-1]]).reshape(P, RC),
        "key_b": key.reshape(BLOCKS, EB), "attr_r": attr.T.reshape(4, P, RC).transpose(1, 0, 2),
        "ew_l": by_tile(attr[:, 3]), "ident": np.eye(P, dtype=np.float32),
        "w_t": np.asarray(L0_gnn_weight)[0].T, "w_pre": np.asarray(L0_gnn_W_pre), "w_post": np.asarray(L0_gnn_W_post),
        "wih_t": w_ih.T, "whh_t": w_hh.T,
        "we_t": np.concatenate([np.asarray(L0_gnn_W_e), np.asarray(L0_gnn_b_e)[None]]).T,
        "b_pre": np.asarray(L0_gnn_b_pre)[None], "b_post": np.asarray(L0_gnn_b_post)[:, None],
        "bih_c": b_ih.reshape(3, C).T, "bhh_c": b_hh.reshape(3, C).T, "bih_r": b_ih[None], "bhh_r": b_hh[None],
        "deg_hist": np.asarray(L0_gnn_deg_hist),
    }
    arrays = {k: np.ascontiguousarray(v) for k, v in arrays.items()}
    nc = bacc.Bacc("TRN2", target_bir_lowering=False, num_devices=1)
    args = {k: nc.dram_tensor("in_" + k, v.shape, mybir.dt.from_np(v.dtype), kind="ExternalInput").ap()
            for k, v in arrays.items()}
    out = nc.dram_tensor("out", (NODES, C), mybir.dt.float32, kind="ExternalOutput").ap()
    gnn_kernel(nc, out=out, **args)
    r = run_bass_kernel_spmd(nc, [{"in_" + k: v for k, v in arrays.items()}], core_ids=[0])
    return r.results[0]["out"]
```

```python
import concourse.bass as bass
from concourse import mybir
from contextlib import ExitStack

NODES, C, EDGES = 100000, 64, 25000
P = 128
BLOCKS = 25
GROUPS = 32
ROWS = P * GROUPS
STRIDE = (NODES - ROWS) // (BLOCKS - 1)
CHUNKS = 4
GC = GROUPS // CHUNKS
TILES = 8
EB = P * TILES
HALF = EB // 2
LAST_TILES = -(-(EDGES - (BLOCKS - 1) * EB) // P)
TH = TILES // 2
ALL_TILES = BLOCKS * TILES
EDGES_PADDED = BLOCKS * EB
RC = EDGES_PADDED // P
OUT_OF_RANGE = 1 << 20
BIG = 1.5e38
EPS = 1e-5
PARTS = 3
AR = 5
KEEP_ROW = PARTS * PARTS * AR
PER_STEP = 29
assert LAST_TILES == TH
assert STRIDE * (BLOCKS - 1) + ROWS == NODES and EDGES <= EDGES_PADDED


ROW_PARTS = {"EW": ALL_TILES, "WIH2": 3 * C, "WHH2": 3 * C, "OW1": 3 * C, "OW2": 3 * C, "BIC": 3, "BHC": 3}
CHANNEL_PARTS = {"WT2": 2 * C, "WPRE": 3 * C, "WP0": C, "STDW": 3 * C, "WIHD": 6 * C, "WET": 4, "BPC": 1}
ROW_COLS, CHANNEL_COLS = sum(ROW_PARTS.values()), sum(CHANNEL_PARTS.values())


def split_columns(tile, widths):
    parts, start = {}, 0
    for name, width in widths.items():
        parts[name] = tile[:, start:start + width]
        start += width
    return parts


class At:

    def __init__(self, j, off):
        self.j, self.off = j, off

    def times(self, per, plus=0):
        c = per * self.off + plus
        return c if self.j is None else self.j * (2 * per) + c

    def pair(self, per):
        c = per * (self.off // 2 + 1)
        return c if self.j is None else self.j * per + c

    def next(self, n=1):
        return At(self.j, self.off + n)

    @property
    def par(self):
        return self.off % 2


def wait(e, sem, value):
    if isinstance(value, int) and value <= 0:
        return
    e.wait_ge(sem, value)


def gnn_kernel(nc, x, gidx, keys, key_b, attr_r, by_row, by_channel, biases, b_pre, deg_hist, ident, out):
    f32, bf16, i32 = mybir.dt.float32, mybir.dt.bfloat16, mybir.dt.int32
    ALU, ACT, AX = mybir.AluOpType, mybir.ActivationFunctionType, mybir.AxisListType.X

    ctx = ExitStack()
    with ctx:
        def sb(name, shape, dt=f32):
            return ctx.enter_context(nc.sbuf_tensor(name, shape, dt))

        def pb(name, shape):
            return ctx.enter_context(nc.psum_tensor(name, shape, f32))

        def sem(name):
            return ctx.enter_context(nc.semaphore(name))

        cnt_rows = nc.dram_tensor("cnt_rows", (P, RC), f32, kind="Internal").ap()
        keep_rows = nc.dram_tensor("keep_rows", (P, RC), bf16, kind="Internal").ap()
        attr_rows = nc.dram_tensor("attr_rows", (PARTS * AR, P, RC), bf16, kind="Internal").ap()
        wau_rows = nc.dram_tensor("wau_rows", (AR, PARTS, C), bf16, kind="Internal").ap()
        late_cell = nc.dram_tensor("late_cell", (BLOCKS, 1), i32, kind="Internal").ap()
        parked = nc.dram_tensor("parked", (BLOCKS, P, TILES * C), f32, kind="Internal").ap()
        bias_rows = nc.dram_tensor("bias_rows", (1, PARTS, 4 * C), bf16, kind="Internal").ap()

        GIDX = sb("GIDX", [P, ALL_TILES * 2], i32)
        SIDX = sb("SIDX", [P, ALL_TILES], i32)
        COEFS = sb("COEFS", [P, ALL_TILES, 4])
        ID = sb("ID", [P, P])
        DW = sb("DW", [P, 4, P])
        DB = sb("DB", [P, 4])
        QW = sb("QW", [P, P])
        WAUG = sb("WAUG", [P, P], bf16)
        SELK = sb("SELK", [P, P], bf16)
        ROWP = sb("ROWP", [P, ROW_COLS])
        parts = split_columns(ROWP, ROW_PARTS)
        EW, WIH2, WHH2, BIC, BHC = (parts[n] for n in ("EW", "WIH2", "WHH2", "BIC", "BHC"))
        OW1 = parts["OW1"]
        OW2 = parts["OW2"]
        SW = sb("SW", [P, 4 * C])
        SBIAS = sb("SBIAS", [P, 2, 4 * C], bf16)
        ONESB = sb("ONESB", [P, P], bf16)
        ATT = [sb(f"ATT{i}", [P, EB], bf16) for i in range(2)]

        X = [sb(f"X{i}", [P, GROUPS, C]) for i in range(2)]
        XN = [sb(f"XN{i}", [P, GROUPS, C]) for i in range(2)]
        OUT = sb("OUT", [P, GROUPS, C])
        SQ = sb("SQ", [P, GROUPS, C])
        HT = [sb(f"HT{i}", [P, 512]) for i in range(2)]
        SR = [sb(f"SR{i}", [P, 512]) for i in range(2)]
        SZ = [sb(f"SZ{i}", [P, 512]) for i in range(2)]
        T = sb("T", [P, 512])
        U = [sb(f"U{i}", [P, 512]) for i in range(2)]
        NN = [sb(f"NN{i}", [P, 512]) for i in range(2)]
        D = sb("D", [P, 512])
        Y = [sb(f"Y{i}", [P, 512]) for i in range(2)]
        SUM = sb("SUM", [P, GROUPS + 2 * TILES])
        MEAN = sb("MEAN", [P, GROUPS + 2 * TILES])
        SSQ = sb("SSQ", [P, GROUPS + 2 * TILES])
        VAR = sb("VAR", [P, GROUPS + 2 * TILES])
        RSTD = sb("RSTD", [P, GROUPS + 2 * TILES])

        IX = [sb(f"IX{i}", [P, 2 * TILES], i32) for i in range(2)]
        XG = [sb(f"XG{i}", [P, TILES, 2, C]) for i in range(2)]
        EC = sb("EC", [P, TILES, 2, C])
        ESQ = sb("ESQ", [P, TILES * 2, C])
        RW = sb("RW", [P, TILES, 2])
        V = sb("V", [P, TILES, 2 * C])
        HO = [sb(f"HO{i}", [P, TILES, 2 * C]) for i in range(2)]
        XD = [sb(f"XD{i}", [P, TILES, C]) for i in range(2)]
        COEF = [sb(f"COEF{i}", [P, TILES, 4]) for i in range(2)]
        VTS = sb("VTS", [P, EB])
        H = sb("H", [P, HALF])
        CAP = sb("CAP", [P, HALF])
        S = sb("S", [P, EB])
        MX = [sb(f"MX{i}", [P, EB]) for i in range(2)]
        MS = sb("MS", [P, TILES, 2 * C])
        M2 = sb("M2", [P, TILES, C])
        MST = sb("MST", [P, EB])
        T1 = sb("T1", [P, TH, 2 * C])
        OS = sb("OS", [P, TH, C])
        HOT = sb("HOT", [P, EB])
        RZ = sb("RZ", [P, TILES, 2 * C])
        TG = sb("TG", [P, TH, C])
        UG = sb("UG", [P, TILES, C])
        NG = sb("NG", [P, TILES, C])
        DG = sb("DG", [P, TILES, C])
        RES = [sb(f"RES{i}", [P, TILES, C]) for i in range(2)]
        SIX = [sb(f"SIX{i}", [P, TILES], i32) for i in range(2)]

        TIN = pb("TIN", [P, 512])
        TOUT = pb("TOUT", [P, 512])
        GATE = pb("GATE", [P, 4, 512])
        EP = pb("EP", [P, EB])
        EPT = EP[:, :].rearrange("p (t c) -> p t c", c=2 * C)
        EPW = EP[:, :].rearrange("p (t c) -> p t c", c=4 * C)

        KEYS = sb("KEYS", [P, 4, RC], i32)
        KL, NL, KR, PR = (KEYS[:, k, :] for k in range(4))
        spare = XN[1][:, :, :].rearrange("p g c -> p (g c)")
        AR_IN = spare[:, 0:4 * RC].rearrange("p (k c) -> p k c", k=4)
        W0 = sb("W0", [P, ALL_TILES])
        W1 = sb("W1", [P, ALL_TILES])
        W2 = sb("W2", [P, ALL_TILES])
        LATE = sb("LATE", [1, BLOCKS + 1], i32)
        LATEC = sb("LATEC", [BLOCKS, 4])
        LATEI = sb("LATEI", [BLOCKS, 1], i32)
        KB = HOT[0:BLOCKS, :].bitcast(i32)
        KBF = RZ[0:BLOCKS, :, :].rearrange("p t c -> p (t c)")
        IDX = sb("IDX", [P, RC])
        KEEP = sb("KEEP", [P, RC], bf16)
        LOC = sb("LOC", [P, RC])
        CARRY = sb("CARRY", [1, P + 1])
        LAST = sb("LAST", [P, 1])
        CNT_R = sb("CNT_R", [P, RC])
        CNT_T = sb("CNT_T", [RC // 2, 2, P])
        AE = spare[:, 4 * RC:(4 + AR) * RC].rearrange("p (k c) -> p k c", k=AR)
        APART = X[1][:, :, :].rearrange("p g c -> p (g c)").bitcast(bf16)[:, 0:PARTS * AR * RC]\
            .rearrange("p (i k c) -> p i k c", i=PARTS, k=AR)
        ONE = sb("ONE", [P, 1])
        CHP = sb("CHP", [C, CHANNEL_COLS])
        parts = split_columns(CHP, CHANNEL_PARTS)
        WT2 = parts["WT2"].rearrange("k (a c) -> k a c", c=C)
        WPRE = parts["WPRE"].rearrange("k (a c) -> k a c", c=C)
        STDW = parts["STDW"].rearrange("k (a c) -> k a c", c=C)
        WIHD = parts["WIHD"].rearrange("k (g a c) -> k g a c", g=3, c=C)
        WP0, WET, BPC = parts["WP0"], parts["WET"], parts["BPC"]
        WAU = sb("WAU", [AR, C])
        WAUR = sb("WAUR", [AR, C])
        WAUP = sb("WAUP", [AR, PARTS, C], bf16)
        BV = sb("BV", [C, 1])
        BIHH = sb("BIHH", [1, 6 * C])
        BIR, BHR = BIHH[:, 0:3 * C], BIHH[:, 3 * C:6 * C]
        BROW = sb("BROW", [1, 4 * C])
        BRES = sb("BRES", [1, 4 * C])
        BPART = sb("BPART", [1, PARTS, 4 * C], bf16)
        DH = sb("DH", [P, 11])
        LDH = sb("LDH", [P, 11])
        AVG = sb("AVG", [P, 1])
        IAVG = sb("IAVG", [P, 1])
        LG = sb("LG", [P, ALL_TILES])
        ILG = sb("ILG", [P, ALL_TILES])
        NOEDGE = sb("NOEDGE", [P, 8])
        M1D = sb("M1D", [C, 2, C])

        names = """index_loaded setup_loaded ident_loaded zeroed flags_made iota_made logs_ready split_saved split_loaded
            prep prep_ready cnt_saved cnt_loaded weights_ready chain chain_act tables_ready
            x_loaded0 x_loaded1 stored0 stored1 blocks_final att_loaded0 att_loaded1
            td_done td_copied gates_done sig_r sig_z t_u tanh_d y_ready to_done out_done
            edge_means_ready row_means_ready xc_ready ec_ready edge_squares row_squares var_ready sd_ready
            xn_done xn_scaled norm_done h_kept xd_kept
            vt_done vt_copied qk_done qk_evac scan_done st_done ms_read v_ready std_ready
            t2_done t2_copied o_done od_done t3_done t3_copied g_done sig_g gru_u tanh_g mix_done res_done
            gathered0 gathered1 scattered0 scattered1 
            late_made late_saved late_loaded any_late park_loaded park_index park_done
            gather_index scatter_index count_seen""".split()
        q = {n: sem(n) for n in names}
        x_loaded, stored, att_loaded, gathered, scattered = (
            [q[n + "0"], q[n + "1"]] for n in ("x_loaded", "stored", "att_loaded", "gathered", "scattered"))

        def rows(t, start):
            return t[bass.ds(start, ROWS), :].rearrange("(p g) c -> p g c", p=P)

        loads = [
            (CHP[:, :], by_channel), (ROWP[:, :], by_row), (DH[:, :], deg_hist.partition_broadcast(P)),
            (BIHH[:, :], biases), (WAU[AR - 1:AR, :], b_pre), (KEYS[:, :, :], keys), (AR_IN[:, :, :], attr_r), (KB, key_b),
        ]
        SETUP_LOADS = 16 * len(loads)
        block = ctx.enter_context(nc.Block())

        def spread(ap, n):
            return ap.unsqueeze(len(ap.shape)).to_broadcast(list(ap.shape) + [n])

        SCALED = GC
        E0 = GROUPS
        E1 = GROUPS + 2 * TILES

        @block.sync
        def _(sp):
            sp.dma_start(GIDX[:, :], gidx).then_inc(q["index_loaded"], 16)
            sp.dma_start(X[0][:, :, :], rows(x, 0)).then_inc(x_loaded[0], 16)
            sp.dma_start(ID[:, :], ident).then_inc(q["ident_loaded"], 16)
            for to, of in loads:
                sp.dma_start(to, of).then_inc(q["setup_loaded"], 16)
            sp.wait_ge(q["flags_made"], 1)
            sp.dma_start(wau_rows, WAUP[:, :, :]).then_inc(q["split_saved"], 16)
            sp.wait_ge(q["flags_made"], 2)
            sp.dma_start(bias_rows, BPART[:, :, :]).then_inc(q["split_saved"], 16)
            sp.wait_ge(q["split_saved"], 32)
            sp.wait_ge(q["zeroed"], 1)
            n = 0
            for j in range(PARTS):
                for i in range(PARTS):
                    at = (j * PARTS + i) * AR
                    sp.dma_start(WAUG[at:at + AR, 0:C], wau_rows[:, j, :]).then_inc(q["split_loaded"], 16)
                    n += 1
            for a in range(2):
                sp.dma_start(SBIAS[0:PARTS, a, :], bias_rows[0, :, :]).then_inc(q["split_loaded"], 16)
                n += 1
            assert n == 11
            sp.wait_ge(q["flags_made"], 3)
            sp.dma_start(keep_rows, KEEP[:, :]).then_inc(q["split_saved"], 16)
            sp.wait_ge(q["flags_made"], 4)
            sp.dma_start(cnt_rows, CNT_R[:, :]).then_inc(q["cnt_saved"], 16)
            sp.wait_ge(q["cnt_saved"], 16)
            counts = cnt_rows.rearrange("p c -> (p c)").rearrange("(a t p) -> t a p", a=2, p=P)
            sp.dma_start(CNT_T[:, :, :], counts).then_inc(q["cnt_loaded"], 16)
            sp.wait_ge(q["flags_made"], 5)
            sp.dma_start(attr_rows.rearrange("k p c -> p k c"), APART[:, :, :, :].rearrange("p i k c -> p (i k) c"))\
                .then_inc(q["split_saved"], 16)
            sp.wait_ge(q["split_saved"], 64)

            keep_flat = keep_rows.rearrange("p c -> (p c)").rearrange("(a n) -> a n", a=1)
            attr_flat = attr_rows.rearrange("k p c -> k (p c)")

            def load_attributes(b):
                start = b.times(EB)
                start = start if isinstance(start, int) else sp.snap(start)
                wait(sp, q["qk_done"], b.next(-1).times(2))
                for j in range(PARTS):
                    sp.dma_start(ATT[b.par][j * PARTS * AR:(j + 1) * PARTS * AR, :], attr_flat[:, bass.ds(start, EB)])\
                        .then_inc(att_loaded[b.par], 16)
                sp.dma_start(ATT[b.par][KEEP_ROW:KEEP_ROW + 1, :], keep_flat[:, bass.ds(start, EB)])\
                    .then_inc(att_loaded[b.par], 16)

            def load_next(i):
                then = i.next().times(STRIDE)
                then = then if isinstance(then, int) else sp.snap(then)
                sp.dma_start(X[1 - i.par][:, :, :], rows(x, then)).then_inc(x_loaded[1 - i.par], 16)
                load_attributes(i.next())

            def step(i, more=True):
                here = i.times(STRIDE)
                here = here if isinstance(here, int) else sp.snap(here)
                if more:
                    load_next(i)
                if i.j is not None or i.off > 0:
                    sp.wait_ge(stored[1 - i.par], i.next(-1).pair(16))
                    sp.sem_inc(q["blocks_final"], 1)
                sp.wait_ge(q["out_done"], i.times(CHUNKS, CHUNKS))
                sp.dma_start(rows(out, here), OUT[:, :, :]).then_inc(stored[i.par], 16)

            load_attributes(At(None, 0))
            load_next(At(None, 0))
            step(At(None, 0), more=False)
            sp.wait_ge(q["late_made"], 1)
            sp.dma_start(late_cell, LATEI[:, :]).then_inc(q["late_saved"], 16)
            sp.wait_ge(q["late_saved"], 16)
            sp.dma_start(LATE[0:1, 0:BLOCKS], late_cell.rearrange("b a -> a b")).then_inc(q["late_loaded"], 16)
            step(At(None, 1))
            with sp.Fori(0, (BLOCKS - 3) // 2) as j:
                step(At(j, 2))
                step(At(j, 3))
            step(At(None, BLOCKS - 1), more=False)
            sp.wait_ge(stored[0], At(None, BLOCKS - 1).pair(16))
            sp.sem_inc(q["blocks_final"], 1)

        @block.gpsimd
        def _(pool):
            pool.memset(ATT[0][:, :], 0.0)
            pool.memset(ATT[1][:, :], 0.0)
            pool.memset(WAUG[:, :], 0.0)
            pool.memset(SBIAS[:, :, :], 0.0)
            pool.memset(ONESB[:, :], 1.0)
            pool.memset(SELK[:, :], 0.0)
            pool.memset(DW[:, :, :], 0.0)
            pool.memset(SW[:, :], 0.0)
            pool.memset(CARRY[:, :], 0.0)
            pool.memset(ONE[:, :], 1.0).then_inc(q["zeroed"], 1)
            pool.wait_ge(q["zeroed"], 1)
            pool.affine_select(out=SELK[:, :], in_=SELK[:, :], compare_op=ALU.not_equal, fill=1.0, base=-KEEP_ROW,
                               pattern=[[0, P]], channel_multiplier=1)
            pool.iota(IDX[:, :], pattern=[[1, RC]], base=0, channel_multiplier=RC,
                      allow_small_or_imprecise_dtypes=True)
            pool.iota(LATEC[:, 1:2], pattern=[[1, 1]], base=2 * STRIDE, channel_multiplier=STRIDE,
                      allow_small_or_imprecise_dtypes=True).then_inc(q["iota_made"], 1)
            pool.wait_ge(q["index_loaded"], 16)

            bound = pool.to_reg(NODES - 1)

            def seen(sem, count):
                wait(pool, sem, count)
                pool.sem_inc(q["count_seen"], 1)

            FIRST = 5

            def gather(b, part):
                if part == 0:
                    at = b.times(2 * TILES)
                    at = at if isinstance(at, int) else pool.snap(at)
                    pool.tensor_copy(IX[b.par][:, :], GIDX[:, bass.ds(at, 2 * TILES)]).then_inc(q["gather_index"], 1)
                    if b.j is not None or b.off > 1:
                        keep_x(b.next(-2))
                        seen(q["xd_kept"], b.times(1, -1))
                    seen(q["gather_index"], b.times(1, 1))
                for t in range(TILES)[:FIRST] if part == 0 else range(TILES)[FIRST:]:
                    for w in range(2):
                        pool.indirect_dma_start(
                            XG[b.par][:, t, w, :], None, x,
                            bass.IndirectOffsetOnAxis(IX[b.par][:, 2 * t + w:2 * t + w + 1], 0),
                            bounds_check=bound, oob_is_err=False).then_inc(gathered[b.par], 16)

            def keep_x(b):
                pool.tensor_copy(XD[b.par][:, :, :], XG[b.par][:, :, 0, :]).then_inc(q["xd_kept"], 1)

            def centre_edges(b):
                seen(q["edge_means_ready"], b.times(1, 1))
                wait_h = b.times(1)
                if not (isinstance(wait_h, int) and wait_h <= 0):
                    seen(q["h_kept"], wait_h)
                pool.tensor_tensor(EC[:, :, :, :].rearrange("p t w c -> p (t w) c"),
                                   XG[b.par][:, :, :, :].rearrange("p t w c -> p (t w) c"),
                                   spread(MEAN[:, E0:E1], C), ALU.subtract).then_inc(q["ec_ready"], 1)

            def centre_rows(b):
                seen(q["row_means_ready"], b.times(1, 1))
                wait_td = b.next(-1).times(CHUNKS)
                if not (isinstance(wait_td, int) and wait_td <= 0):
                    seen(q["td_done"], wait_td)
                pool.tensor_tensor(XN[b.par][:, :, :], X[b.par][:, :, :], spread(MEAN[:, 0:E0], C), ALU.subtract)\
                    .then_inc(q["xc_ready"], 1)

            def finish(b, tiles=TILES):
                if b.j is not None or b.off > 1:
                    seen(scattered[b.par], b.next(-2).pair(16 * TILES))
                seen(q["xd_kept"], b.times(1, 1))
                seen(q["mix_done"], b.times(1, 1))
                pool.tensor_tensor(RES[b.par][:, 0:tiles, :], DG[:, 0:tiles, :], XD[b.par][:, 0:tiles, :], ALU.add)\
                    .then_inc(q["res_done"], 1)
                seen(q["res_done"], b.times(1, 1))

            def scatter(b, final=False, tiles=TILES):
                at = b.times(TILES)
                at = at if isinstance(at, int) else pool.snap(at)
                pool.tensor_copy(SIX[b.par][:, :], SIDX[:, bass.ds(at, TILES)]).then_inc(q["scatter_index"], 1)
                seen(q["scatter_index"], b.times(1, 1))
                seen(q["blocks_final"], BLOCKS if final else b.times(1, 2))
                send(b, tiles)

            def rows_to_out(index, results, done, tiles=TILES):
                for t in range(tiles):
                    pool.indirect_dma_start(
                        out, bass.IndirectOffsetOnAxis(index[:, t:t + 1], 0), results[:, t, :], None,
                        bounds_check=bound, oob_is_err=False).then_inc(done, 16)

            def send(b, tiles):
                number = b.times(1)
                number = number if isinstance(number, int) else pool.snap(number)
                with pool.If(any_late > 0):
                    for t in range(TILES):
                        pool.dma_start(parked[bass.ds(number, 1), :, C * t:C * t + C].rearrange("a p c -> p (a c)"),
                                       RES[b.par][:, t, :]).then_inc(scattered[b.par], 16)
                with pool.Else():
                    rows_to_out(SIX[b.par], RES[b.par], scattered[b.par], tiles)

            def step(i, rows=True, more=True, ends=True):
                if ends:
                    finish(i.next(-2))
                if more:
                    gather(i.next(2), 0)
                else:
                    keep_x(i)
                if rows:
                    centre_edges(i.next())
                    centre_rows(i.next())
                if ends:
                    scatter(i.next(-2))
                if more:
                    gather(i.next(2), 1)

            gather(At(None, 0), 0)
            centre_rows(At(None, 0))
            gather(At(None, 0), 1)
            centre_edges(At(None, 0))
            gather(At(None, 1), 0)
            gather(At(None, 1), 1)
            step(At(None, 0), ends=False)
            step(At(None, 1), ends=False)
            pool.wait_ge(q["tables_ready"], 1)
            pool.wait_ge(q["any_late"], 1)
            any_late = pool.value_load(LATE[0:1, BLOCKS:BLOCKS + 1], min_val=0, max_val=1)
            with pool.Fori(0, (BLOCKS - 5) // 2) as j:
                step(At(j, 2))
                step(At(j, 3))
            step(At(None, BLOCKS - 3))
            step(At(None, BLOCKS - 2), more=False)
            before_last, last = At(None, BLOCKS - 2), At(None, BLOCKS - 1)
            finish(At(None, BLOCKS - 3))
            scatter(At(None, BLOCKS - 3))
            keep_x(last)
            finish(before_last)
            scatter(before_last, final=True)
            finish(last, LAST_TILES)
            scatter(last, final=True, tiles=LAST_TILES)
            with pool.If(any_late > 0):
                for par in range(2):
                    pool.wait_ge(scattered[par], 16 * TILES * ((BLOCKS + 1 - par) // 2))
                with pool.Fori(0, BLOCKS) as b:
                    at = pool.snap(b * TILES)
                    pool.tensor_copy(SIX[0][:, :], SIDX[:, bass.ds(at, TILES)]).then_inc(q["park_index"], 1)
                    pool.dma_start(RES[0][:, :, :].rearrange("p t c -> p (t c)"),
                                   parked[bass.ds(b, 1), :, :].rearrange("a p c -> p (a c)")).then_inc(q["park_loaded"], 16)
                    pool.wait_ge(q["park_index"], b + 1)
                    pool.sem_inc(q["count_seen"], 1)
                    pool.wait_ge(q["park_loaded"], b * 16 + 16)
                    pool.sem_inc(q["count_seen"], 1)
                    rows_to_out(SIX[0], RES[0], q["park_done"])
                    pool.wait_ge(q["park_done"], b * (16 * TILES) + 16 * TILES)
                    pool.sem_inc(q["count_seen"], 1)
            with pool.Else():
                pool.wait_ge(scattered[0], 16 * (TILES * ((BLOCKS + 1) // 2 - 1) + LAST_TILES))
                pool.wait_ge(scattered[1], 16 * TILES * (BLOCKS // 2))

        @block.vector
        def _(dve):
            done = [0]
            base = [At(None, 0), 0]

            def chained(ins):
                ins.then_inc(q["chain"], 1)
                done[0] += 1

            def settle():
                dve.wait_ge(q["chain"], base[0].times(PER_STEP, base[1] + done[0]))

            def link(ins):
                chained(ins)
                settle()

            made = {}

            def making(name, ins):
                chained(ins)
                made[name] = done[0]

            def after(*names):
                dve.wait_ge(q["chain"], base[0].times(PER_STEP, base[1] + max(made[name] for name in names)))

            tt, ts, stt, copy = dve.tensor_tensor, dve.tensor_scalar, dve.scalar_tensor_tensor, dve.tensor_copy

            def edge_sums(b):
                dve.wait_ge(gathered[b.par], b.pair(16 * 2 * TILES))
                xg = XG[b.par][:, :, :, :].rearrange("p t w c -> p (t w) c")
                making("sum_e", dve.tensor_reduce(SUM[:, E0:E1], xg, AX, ALU.add))

            def edge_means(b):
                after("sum_e")
                ts(MEAN[:, E0:E1], SUM[:, E0:E1], 1.0 / C, None, ALU.mult).then_inc(q["edge_means_ready"], 1)

            def row_sums(b):
                dve.wait_ge(x_loaded[b.par], b.pair(16))
                making("sum", dve.tensor_reduce(SUM[:, 0:E0], X[b.par][:, :, :], AX, ALU.add))

            def row_means(b):
                after("sum")
                ts(MEAN[:, 0:E0], SUM[:, 0:E0], 1.0 / C, None, ALU.mult).then_inc(q["row_means_ready"], 1)

            def edge_squares(b):
                dve.wait_ge(q["edge_squares"], b.times(1, 1))
                making("ssq_e", dve.tensor_reduce(SSQ[:, E0:E1], ESQ[:, :, :], AX, ALU.add))

            def row_squares(b):
                dve.wait_ge(q["row_squares"], b.times(1, 1))
                making("ssq", dve.tensor_reduce(SSQ[:, 0:E0], SQ[:, :, :], AX, ALU.add))

            def variance(b):
                after("ssq", "ssq_e")
                ts(VAR[:, :], SSQ[:, :], 1.0 / C, EPS, ALU.mult, ALU.add).then_inc(q["var_ready"], 1)

            def rstd(b):
                dve.wait_ge(q["sd_ready"], b.times(1, 1))
                wait(dve, q["xn_scaled"], b.times(CHUNKS - SCALED // GC))
                making("rstd", dve.reciprocal(RSTD[:, :], VAR[:, :]))

            def normalise(b):
                after("rstd")
                xn = XN[b.par][:, 0:SCALED, :]
                tt(xn, xn, spread(RSTD[:, 0:SCALED], C), ALU.mult).then_inc(q["xn_done"], 1)

            def coefficients(b):
                at = b.times(TILES)
                at = at if isinstance(at, int) else dve.snap(at)
                making("coef", ts(COEF[b.par][:, :, :], COEFS[:, bass.ds(at, TILES), :], 1.0, None, ALU.mult))

            def weights(b):
                after("coef")
                rs = RSTD[:, E0:E1].rearrange("p (t w) -> p t w", w=2)
                making("rw", tt(RW[:, :, :], rs, spread(COEF[b.par][:, :, 3], 2), ALU.mult))

            def weighted(b):
                after("rw")
                wait(dve, q["vt_done"], b.times(2))
                stt(V[:, :, :].rearrange("p t (w c) -> p t w c", w=2), EC[:, :, :, :], 0.0, spread(RW[:, :, :], C),
                    ALU.max, ALU.mult).then_inc(q["norm_done"], 1)

            def keep_h(b):
                stt(HO[b.par][:, :, 0:C], EC[:, :, 0, :], 0.0,
                    spread(RSTD[:, E0:E1].rearrange("p (t w) -> p t w", w=2)[:, :, 0], C), ALU.max, ALU.mult)\
                    .then_inc(q["h_kept"], 1)

            def reset_n(i, c):
                dve.wait_ge(q["sig_r"], i.times(CHUNKS, c + 1))
                dve.wait_ge(q["gates_done"], i.times(4 * CHUNKS, 4 * c + 3))
                making("t", stt(T[:, :], GATE[:, 2, :], DB[:, 2:3], SR[c % 2][:, :], ALU.add, ALU.mult))

            def input_n(i, c):
                after("t")
                dve.wait_ge(q["gates_done"], i.times(4 * CHUNKS, 4 * c + 4))
                wait(dve, q["tanh_d"], i.times(CHUNKS, c - 1))
                tt(U[c % 2][:, :], T[:, :], GATE[:, 3, :], ALU.add).then_inc(q["t_u"], 1)

            def mix_less(i, c):
                dve.wait_ge(q["tanh_d"], i.times(CHUNKS, c + 1))
                making("d", tt(D[:, :], HT[c % 2][:, :], NN[c % 2][:, :], ALU.subtract))

            def mix_times(i, c):
                after("d")
                dve.wait_ge(q["sig_z"], i.times(CHUNKS, c + 1))
                making("d", tt(D[:, :], D[:, :], SZ[c % 2][:, :], ALU.mult))

            def mix_plus(i, c):
                after("d")
                wait(dve, q["to_done"], i.times(CHUNKS, c - 1))
                tt(Y[c % 2][:, :], D[:, :], NN[c % 2][:, :], ALU.add).then_inc(q["y_ready"], 1)

            def add_x(i, c):
                dve.wait_ge(q["to_done"], i.times(CHUNKS, c + 1))
                if c == 0 and (i.j is not None or i.off > 0):
                    dve.wait_ge(stored[1 - i.par], i.next(-1).pair(16))
                groups = slice(GC * c, GC * c + GC)
                tt(OUT[:, groups, :].rearrange("p g c -> p (g c)"), X[i.par][:, groups, :].rearrange("p g c -> p (g c)"),
                   TOUT[:, :], ALU.add).then_inc(q["out_done"], 1)

            def scan(i, h):
                cols = slice(HALF * h, HALF * h + HALF)
                dve.wait_ge(q["qk_evac"], i.times(2, h + 1))
                wait(dve, q["st_done"], i.times(1))
                wait(dve, q["o_done"], i.next(-1).times(2))
                first = h == 0 and i.j is None and i.off == 0
                before = EB - 1 if h == 0 else HALF - 1
                s0 = 0.0 if first else S[:, before:before + 1]
                m0 = -BIG if first else MX[i.par if h else 1 - i.par][:, before:before + 1]
                dve.tensor_tensor_scan(S[:, cols], EP[:, HALF:EB], H[:, :], s0, ALU.mult, ALU.add)
                dve.tensor_tensor_scan(MX[i.par][:, cols], CAP[:, :], EP[:, 0:HALF], m0, ALU.min, ALU.max)\
                    .then_inc(q["scan_done"], 1)

            def means(i):
                dve.wait_ge(q["st_done"], i.times(1, 1))
                wait(dve, q["t2_done"], i.times(2))
                tt(MS[:, :, :], EPT, spread(COEF[i.par][:, :, 0], P), ALU.mult).then_inc(q["ms_read"], 1)

            def means_squared(i):
                dve.wait_ge(q["ms_read"], i.times(1, 1))
                making("m2", tt(M2[:, :, :], MS[:, :, 0:C], MS[:, :, 0:C], ALU.mult))

            def variances(i):
                after("m2")
                making("v", tt(MS[:, :, C:P], MS[:, :, C:P], M2[:, :, :], ALU.subtract))

            def variances_up(i):
                after("v")
                ts(MS[:, :, C:P], MS[:, :, C:P], 0.0, EPS, ALU.max, ALU.add).then_inc(q["v_ready"], 1)

            def post_scaled(b, h):
                tiles = slice(TH * h, TH * h + TH)
                dve.wait_ge(q["o_done"], b.times(2, h + 1))
                t1 = T1[:, :, :].rearrange("p t (k c) -> p t k c", k=2)
                making("t1", tt(t1, EPW[:, :, C:3 * C].rearrange("p t (k c) -> p t k c", k=2),
                                spread(COEF[b.par][:, tiles, 1:3], C), ALU.mult))

            def post_sum(b, h):
                after("t1")
                making("os", tt(OS[:, :, :], T1[:, :, 0:C], T1[:, :, C:P], ALU.add))

            def post_id(b, h):
                tiles = slice(TH * h, TH * h + TH)
                after("os")
                tt(HO[b.par][:, tiles, C:P], OS[:, :, :], EPW[:, :, 0:C], ALU.add).then_inc(q["od_done"], 1)

            def edge_reset_n(b, h):
                tiles = slice(TH * h, TH * h + TH)
                dve.wait_ge(q["sig_g"], b.times(2, h + 1))
                making("tg", tt(TG[:, :, :], EPW[:, :, 2 * C:3 * C], RZ[:, tiles, 0:C], ALU.mult))

            def edge_input_n(b, h):
                tiles = slice(TH * h, TH * h + TH)
                after("tg")
                tt(UG[:, tiles, :], TG[:, :, :], EPW[:, :, 3 * C:4 * C], ALU.add).then_inc(q["gru_u"], 1)

            def edge_mix_less(b, tiles=TILES):
                dve.wait_ge(q["tanh_g"], b.times(2, 2 if tiles == TILES else 1))
                wait(dve, q["res_done"], b.times(1))
                t = slice(0, tiles)
                making("dg", tt(DG[:, t, :], HO[b.par][:, t, 0:C], NG[:, t, :], ALU.subtract))

            def edge_mix_times(b, tiles=TILES):
                t = slice(0, tiles)
                after("dg")
                making("dg", tt(DG[:, t, :], DG[:, t, :], RZ[:, t, C:P], ALU.mult))

            def edge_mix_plus(b, tiles=TILES):
                t = slice(0, tiles)
                after("dg")
                tt(DG[:, t, :], DG[:, t, :], NG[:, t, :], ALU.add).then_inc(q["mix_done"], 1)

            def step(i, new=True, old=True):
                p, n = i.next(-1), i.next()
                done[0] = 0
                reset_n(i, 0)
                if old:
                    add_x(p, 3)
                keep_h(i)
                input_n(i, 0)
                if new:
                    edge_sums(n)
                mix_less(i, 0)
                scan(i, 0)
                if new:
                    edge_means(n)
                reset_n(i, 1)
                mix_times(i, 0)
                mix_plus(i, 0)
                input_n(i, 1)
                if old:
                    post_scaled(p, 0)
                    post_sum(p, 0)
                    post_id(p, 0)
                if new:
                    row_sums(n)
                    row_means(n)
                add_x(i, 0)
                mix_less(i, 1)
                scan(i, 1)
                mix_times(i, 1)
                reset_n(i, 2)
                mix_plus(i, 1)
                input_n(i, 2)
                if old:
                    post_scaled(p, 1)
                    post_sum(p, 1)
                    post_id(p, 1)
                add_x(i, 1)
                means(i)
                if new:
                    edge_squares(n)
                    row_squares(n)
                means_squared(i)
                if new:
                    variance(n)
                variances(i)
                mix_less(i, 2)
                variances_up(i)
                if old:
                    edge_reset_n(p, 0)
                    edge_input_n(p, 0)
                mix_times(i, 2)
                mix_plus(i, 2)
                if new:
                    rstd(n)
                    normalise(n)
                reset_n(i, 3)
                input_n(i, 3)
                if new:
                    coefficients(n)
                if old:
                    edge_reset_n(p, 1)
                if new:
                    weights(n)
                if old:
                    edge_input_n(p, 1)
                if new:
                    weighted(n)
                mix_less(i, 3)
                add_x(i, 2)
                mix_times(i, 3)
                if old:
                    edge_mix_less(p)
                mix_plus(i, 3)
                if old:
                    edge_mix_times(p)
                    edge_mix_plus(p)

            b0 = At(None, 0)
            row_sums(b0)
            row_means(b0)

            dve.wait_ge(q["setup_loaded"], SETUP_LOADS)
            dve.wait_ge(q["prep"], 1)
            copy(QW[0:C, 0:C], GATE[0:C, 1, 0:C])
            ts(QW[0:C, C:P], GATE[0:C, 1, 0:C], -1.0, None, ALU.mult)
            copy(QW[C:P, 0:C], GATE[C:P, 1, C:P])
            ts(QW[C:P, C:P], GATE[C:P, 1, C:P], -1.0, None, ALU.mult)
            copy(M1D[:, 0, :], GATE[0:C, 2, 0:C])
            copy(M1D[:, 1, :], GATE[0:C, 2, 0:C])
            copy(WAU[0:4, :], GATE[0:4, 3, 0:C])
            tt(BROW[:, 0:2 * C], BIR[:, 0:2 * C], BHR[:, 0:2 * C], ALU.add)
            copy(BROW[:, 2 * C:3 * C], BHR[:, 2 * C:3 * C])
            link(copy(BROW[:, 3 * C:4 * C], BIR[:, 2 * C:3 * C]))
            tt(BROW[:, 0:2 * C], BROW[:, 0:2 * C], EP[0:1, 0:2 * C], ALU.add)
            tt(BROW[:, 3 * C:4 * C], BROW[:, 3 * C:4 * C], EP[0:1, 2 * C:3 * C], ALU.add)
            dve.wait_ge(q["logs_ready"], 1)
            link(dve.tensor_reduce(AVG[:, :], LDH[:, :], AX, ALU.add))
            link(ts(AVG[:, :], AVG[:, :], 1.0 / 11, None, ALU.mult))
            dve.reciprocal(IAVG[:, :], AVG[:, :])
            link(dve.reciprocal(NOEDGE[:, 4:5], NOEDGE[:, 3:4]))
            tt(NOEDGE[:, 1:2], NOEDGE[:, 3:4], IAVG[:, :], ALU.mult)
            link(tt(NOEDGE[:, 2:3], NOEDGE[:, 4:5], AVG[:, :], ALU.mult))
            link(tt(NOEDGE[:, 2:3], NOEDGE[:, 2:3], NOEDGE[:, 1:2], ALU.mult))
            link(ts(NOEDGE[:, 1:3], NOEDGE[:, 1:3], EPS ** 0.5, None, ALU.mult))
            link(dve.memset(NOEDGE[:, 0:1], EPS ** 0.5))
            dve.sem_inc(q["prep_ready"], 1)
            for i in range(PARTS):
                link(copy(WAUP[:, i, :], WAU[:, :] if i == 0 else WAUR[:, :]))
                if i < PARTS - 1:
                    link(tt(WAUR[:, :], WAU[:, :] if i == 0 else WAUR[:, :], WAUP[:, i, :], ALU.subtract))
            dve.sem_inc(q["flags_made"], 1)
            for i in range(PARTS):
                link(copy(BPART[:, i, :], BROW[:, :] if i == 0 else BRES[:, :]))
                if i < PARTS - 1:
                    link(tt(BRES[:, :], BROW[:, :] if i == 0 else BRES[:, :], BPART[:, i, :], ALU.subtract))
            dve.sem_inc(q["flags_made"], 1)

            dve.wait_ge(q["iota_made"], 1)
            copy(W2[:, :], KR[:, :])
            link(copy(LOC[:, :], PR[:, :]))
            link(tt(W2[:, :], W2[:, :], LOC[:, :], ALU.is_equal))
            copy(KEEP[:, :], W2[:, :]).then_inc(q["flags_made"], 1)

            link(tt(W2[:, :], W2[:, :], IDX[:, :], ALU.mult))
            link(tt(W2[:, :], IDX[:, :], W2[:, :], ALU.subtract))
            link(dve.tensor_tensor_scan(LOC[:, :], W2[:, :], W2[:, :], 0.0, ALU.max, ALU.max))
            copy(LAST[:, :], LOC[:, RC - 1:RC]).then_inc(q["prep_ready"], 1)
            dve.wait_ge(q["prep"], 2)
            link(tt(BV[:, :], TOUT[0:C, 0:1], BPC[:, :], ALU.add))
            dve.sem_inc(q["prep_ready"], 1)
            dve.wait_ge(q["prep"], 3)
            link(copy(LG[0:1, 0:P], GATE[0:1, 0, 0:P]))
            link(dve.tensor_tensor_scan(CARRY[:, 1:P + 1], LG[0:1, 0:P], LG[0:1, 0:P], 0.0, ALU.max, ALU.max))
            dve.sem_inc(q["prep_ready"], 1)

            for g in range(2):
                for h in range(2):
                    r = slice(C * h, C * h + C)
                    tt(DW[r, g, r], TIN[r, C * g:C * g + C], WHH2[r, C * g:C * g + C], ALU.add)
                copy(SW[C:P, C * g:C * g + C], WIH2[C:P, C * g:C * g + C])
                tt(SW[0:C, C * g:C * g + C], TIN[0:C, C * g:C * g + C], WHH2[0:C, C * g:C * g + C], ALU.add)
            for h in range(2):
                r = slice(C * h, C * h + C)
                copy(DW[r, 2, r], WHH2[r, 2 * C:3 * C])
                copy(DW[r, 3, r], TIN[r, 2 * C:3 * C])
            copy(SW[0:C, 2 * C:3 * C], WHH2[0:C, 2 * C:3 * C])
            copy(SW[0:C, 3 * C:4 * C], TIN[0:C, 2 * C:3 * C])
            copy(SW[C:P, 3 * C:4 * C], WIH2[C:P, 2 * C:3 * C])
            ts(OW2[C:P, :], OW2[C:P, :], -1.0, None, ALU.mult)
            link(tt(BIC[:, 0:2], BIC[:, 0:2], BHC[:, 0:2], ALU.add))
            dve.wait_ge(q["prep"], 4)
            tt(DB[:, 0:2], EP[:, 0:2], BIC[:, 0:2], ALU.add)
            copy(DB[:, 2:3], BHC[:, 2:3])
            link(tt(DB[:, 3:4], EP[:, 2:3], BIC[:, 2:3], ALU.add))
            dve.sem_inc(q["weights_ready"], 1)

            dve.wait_ge(q["prep"], 5)
            link(copy(LAST[:, :], TOUT[:, 0:1]))
            link(stt(W2[:, :], LOC[:, :], LAST[:, 0:1], IDX[:, :], ALU.max, ALU.subtract))
            ts(CNT_R[:, :], W2[:, :], -1.0, 1.0, ALU.mult, ALU.add).then_inc(q["flags_made"], 1)
            edge_sums(b0)
            edge_means(b0)

            ew_r = AR_IN[:, 3, :]
            for k in range(3):
                tt(AE[:, k, :], AR_IN[:, k, :], ew_r, ALU.mult)
            copy(AE[:, 3, :], ew_r)
            link(dve.memset(AE[:, 4, :], 1.0))
            for i in range(PARTS):
                link(copy(APART[:, i, :, :], AE[:, :, :]))
                if i < PARTS - 1:
                    link(tt(AE[:, :, :], AE[:, :, :], APART[:, i, :, :], ALU.subtract))
            dve.sem_inc(q["flags_made"], 1)

            row_squares(b0)
            edge_squares(b0)
            variance(b0)
            rstd(b0)
            normalise(b0)
            dve.wait_ge(q["split_loaded"], 16 * 11)
            link(copy(WAUG[:, C:P], WAUG[:, 0:C]))
            link(ts(WAUG[:, C:P], WAUG[:, 0:C], -1.0, None, ALU.mult))

            dve.wait_ge(q["prep"], 6)
            copy(W0[:, 0:RC // 2], GATE[:, 0, 0:RC // 2])
            link(copy(W0[:, RC // 2:RC], GATE[:, 0, P:P + RC // 2]))
            dve.sem_inc(q["prep_ready"], 1)
            copy(COEFS[:, :, 3], EW[:, :])
            dve.reciprocal(COEFS[:, :, 0], W0[:, :])
            dve.wait_ge(q["logs_ready"], 2)
            dve.reciprocal(ILG[:, :], LG[:, :])
            link(ts(COEFS[:, :, 1], LG[:, :], IAVG[:, 0:1], None, ALU.mult))
            link(ts(ILG[:, :], ILG[:, :], AVG[:, 0:1], None, ALU.mult))
            link(tt(COEFS[:, :, 2], ILG[:, :], COEFS[:, :, 1], ALU.mult))
            dve.sem_inc(q["tables_ready"], 1)
            coefficients(b0)
            weights(b0)
            weighted(b0)
            base[1] = done[0]
            step(At(None, 0), old=False)
            copy(W0[:, :], KL[:, :])
            link(copy(W1[:, :], NL[:, :]))
            link(tt(W1[:, :], W0[:, :], W1[:, :], ALU.is_equal))
            link(stt(W1[:, :], W1[:, :], float(OUT_OF_RANGE), W0[:, :], ALU.mult, ALU.add))
            link(copy(SIDX[:, :], W1[:, :]))

            link(copy(KBF, KB))
            link(dve.tensor_reduce(LATEC[:, 0:1], KBF, AX, ALU.max))
            link(tt(LATEC[:, 2:3], LATEC[:, 0:1], LATEC[:, 1:2], ALU.is_ge))
            copy(LATEI[:, :], LATEC[:, 2:3]).then_inc(q["late_made"], 1)
            at_one = base[1] + done[0]
            base[:] = [At(None, 1), at_one - PER_STEP]
            step(At(None, 1))
            assert done[0] == PER_STEP, done[0]
            dve.wait_ge(q["late_loaded"], 16)
            dve.tensor_reduce(LATE[:, BLOCKS:BLOCKS + 1], LATE[:, 0:BLOCKS - 2], AX, ALU.max).then_inc(q["any_late"], 1)
            with dve.Fori(0, (BLOCKS - 3) // 2) as j:
                for k in range(2):
                    base[0] = At(j, 2 + k)
                    step(At(j, 2 + k))
            base[0] = At(None, BLOCKS - 1)
            step(At(None, BLOCKS - 1), new=False)
            last = At(None, BLOCKS - 1)
            add_x(last, 3)
            post_scaled(last, 0)
            post_sum(last, 0)
            post_id(last, 0)
            edge_reset_n(last, 0)
            edge_input_n(last, 0)
            edge_mix_less(last, LAST_TILES)
            edge_mix_times(last, LAST_TILES)
            edge_mix_plus(last, LAST_TILES)

        @block.scalar
        def _(act):
            def act_on(out_, in_, func, **kw):
                return act.activation(out_, in_, func, **kw)

            act.wait_ge(q["setup_loaded"], SETUP_LOADS)
            act.wait_ge(q["zeroed"], 1)
            act_on(LDH[:, :], DH[:, :], ACT.Ln, bias=ONE[:, 0:1])
            act_on(NOEDGE[:, 3:4], ONE[:, :], ACT.Ln, bias=ONE[:, 0:1]).then_inc(q["logs_ready"], 1)

            def edge_squares(b):
                act.wait_ge(q["ec_ready"], b.times(1, 1))
                wait(act, q["var_ready"], b.times(1))
                act_on(ESQ[:, :, :], EC[:, :, :, :].rearrange("p t w c -> p (t w) c"), ACT.Square)\
                    .then_inc(q["edge_squares"], 1)

            def row_squares(b):
                act.wait_ge(q["xc_ready"], b.times(1, 1))
                wait(act, q["var_ready"], b.times(1))
                act_on(SQ[:, :, :], XN[b.par][:, :, :], ACT.Square).then_inc(q["row_squares"], 1)

            def roots(i, new=True, cur=True):
                if cur:
                    act.wait_ge(q["v_ready"], i.times(1, 1))
                    act_on(MS[:, :, C:P], MS[:, :, C:P], ACT.Sqrt).then_inc(q["std_ready"], 1)
                if new:
                    b = i.next()
                    act.wait_ge(q["var_ready"], b.times(1, 1))
                    act_on(VAR[:, :], VAR[:, :], ACT.Sqrt).then_inc(q["sd_ready"], 1)

            def scale_rows(i, c):
                if c == SCALED // GC:
                    act.wait_ge(q["xn_done"], i.times(1, 1))
                for g in range(GC * c, GC * c + GC):
                    last = act_on(XN[i.par][:, g, :], XN[i.par][:, g, :], ACT.Copy, scale=RSTD[:, g:g + 1])
                last.then_inc(q["xn_scaled"], 1)

            def take_h(i, c):
                act.wait_ge(q["td_done"], i.times(CHUNKS, c + 1))
                wait(act, q["gates_done"], i.times(4 * CHUNKS, 4 * (c - 1)))
                wait(act, q["y_ready"], i.times(CHUNKS, c - 1))
                act_on(HT[c % 2][:, :], TIN[:, :], ACT.Relu).then_inc(q["td_copied"], 1)

            def gates_rz(i, c):
                act.wait_ge(q["gates_done"], i.times(4 * CHUNKS, 4 * c + 1))
                wait(act, q["t_u"], i.times(CHUNKS, c - 1))
                act_on(SR[c % 2][:, :], GATE[:, 0, :], ACT.Sigmoid, bias=DB[:, 0:1]).then_inc(q["sig_r"], 1)
                act.wait_ge(q["gates_done"], i.times(4 * CHUNKS, 4 * c + 2))
                wait(act, q["y_ready"], i.times(CHUNKS, c - 1))
                act_on(SZ[c % 2][:, :], GATE[:, 1, :], ACT.Sigmoid, bias=DB[:, 1:2]).then_inc(q["sig_z"], 1)

            def gate_n(i, c):
                act.wait_ge(q["t_u"], i.times(CHUNKS, c + 1))
                wait(act, q["y_ready"], i.times(CHUNKS, c - 1))
                act_on(NN[c % 2][:, :], U[c % 2][:, :], ACT.Tanh, bias=DB[:, 3:4]).then_inc(q["tanh_d"], 1)

            def messages(i, h):
                act.wait_ge(q["qk_done"], i.times(2, h + 1))
                wait(act, q["scan_done"], i.times(2, h))
                act_on(H[0:C, :], EP[0:C, 0:HALF], ACT.Copy)
                act_on(H[C:P, :], EP[C:P, 0:HALF], ACT.Square)
                act_on(CAP[:, :], EP[:, HALF:EB], ACT.Copy, scale=2 * BIG, bias=-BIG).then_inc(q["qk_evac"], 1)

            def edge_gates_rz(b, h):
                tiles = slice(TH * h, TH * h + TH)
                act.wait_ge(q["g_done"], b.times(2, h + 1))
                wait(act, q["mix_done"], b.times(1))
                act_on(RZ[:, tiles, :], EPW[:, :, 0:2 * C], ACT.Sigmoid).then_inc(q["sig_g"], 1)

            def edge_gate_n(b, h):
                tiles = slice(TH * h, TH * h + TH)
                act.wait_ge(q["gru_u"], b.times(2, h + 1))
                act_on(NG[:, tiles, :], UG[:, tiles, :], ACT.Tanh).then_inc(q["tanh_g"], 1)

            def halves_out(b, to, turned, read, copied, halves=2):
                for h in range(halves):
                    act.wait_ge(turned, b.times(2, h + 1))
                    wait(act, read, b.times(2))
                    cols = slice(HALF * h, HALF * h + HALF)
                    act_on(to[:, cols], EP[:, cols], ACT.Copy).then_inc(copied, 1)

            def take_v(i):
                halves_out(i, VTS, q["vt_done"], q["qk_done"], q["vt_copied"])

            def take_moments(b):
                halves_out(b, MST, q["t2_done"], q["o_done"], q["t2_copied"])

            def take_ho(b, halves=2):
                halves_out(b, HOT, q["t3_done"], q["g_done"], q["t3_copied"], halves)

            def step(i, new=True, old=True):
                p, n = i.next(-1), i.next()
                take_h(i, 1)
                messages(i, 0)
                gate_n(i, 0)
                gates_rz(i, 1)
                scale_rows(i, 2)
                gate_n(i, 1)
                take_h(i, 2)
                scale_rows(i, 3)
                messages(i, 1)
                gates_rz(i, 2)
                if new:
                    edge_squares(n)
                take_h(i, 3)
                if new:
                    row_squares(n)
                if old:
                    take_ho(p)
                gate_n(i, 2)
                if old:
                    edge_gates_rz(p, 0)
                roots(i, new)
                gates_rz(i, 3)
                if old:
                    edge_gate_n(p, 0)
                    edge_gates_rz(p, 1)
                if new:
                    take_h(n, 0)
                gate_n(i, 3)
                if new:
                    scale_rows(n, 1)
                if old:
                    edge_gate_n(p, 1)
                take_moments(i)
                if new:
                    gates_rz(n, 0)
                    take_v(n)

            row_squares(At(None, 0))
            edge_squares(At(None, 0))
            roots(At(None, -1), cur=False)
            act.wait_ge(q["prep_ready"], 5)
            act_on(LG[:, :], W0[:, :], ACT.Ln, bias=ONE[:, 0:1]).then_inc(q["logs_ready"], 1)
            take_h(At(None, 0), 0)
            scale_rows(At(None, 0), 1)
            gates_rz(At(None, 0), 0)
            take_v(At(None, 0))
            step(At(None, 0), old=False)
            step(At(None, 1))
            with act.Fori(0, (BLOCKS - 3) // 2) as j:
                step(At(j, 2))
                step(At(j, 3))
            last = At(None, BLOCKS - 1)
            step(last, new=False)
            take_ho(last, 1)
            edge_gates_rz(last, 0)
            edge_gate_n(last, 0)

        @block.tensor
        def _(pe):
            mm, tr = pe.matmul, pe.transpose
            pe.wait_ge(q["ident_loaded"], 16)
            pe.wait_ge(q["setup_loaded"], SETUP_LOADS)
            pe.wait_ge(q["zeroed"], 1)
            mm(GATE[:, 1, 0:P], WT2[:, :, :].rearrange("k a c -> k (a c)"),
               WPRE[:, 0:2, :].rearrange("k a c -> k (a c)"), start=True, stop=True)
            mm(GATE[0:C, 2, 0:C], WP0[:, :], WT2[:, 0, :], start=True, stop=True)
            mm(GATE[0:4, 3, 0:C], WET[:, :], WPRE[:, 2, :], start=True, stop=True)
            mm(EP[0:1, 0:3 * C], BPC[:, :], WIH2[0:C, :], start=True, stop=True).then_inc(q["prep"], 1)
            pe.wait_ge(q["prep_ready"], 1)
            mm(TIN[:, 0:3 * C], M1D[:, :, :].rearrange("k a c -> k (a c)"), WIH2[0:C, :], start=True, stop=True)
            for k in range(3):
                last = mm(TOUT[0:C, 0:1], STDW[:, k, :], NOEDGE[0:C, k:k + 1], start=k == 0, stop=k == 2)
            last.then_inc(q["prep"], 1)
            pe.wait_ge(q["prep_ready"], 2)
            mm(GATE[0:1, 0, 0:P], LAST[:, :], ID[:, :], start=True, stop=True).then_inc(q["prep"], 1)
            pe.wait_ge(q["prep_ready"], 3)
            for g in range(3):
                last = mm(EP[:, g:g + 1], WIHD[:, g, :, :].rearrange("k a c -> k (a c)"), BV[:, :], start=True, stop=True)
            last.then_inc(q["prep"], 1)
            pe.wait_ge(q["prep_ready"], 4)
            mm(TOUT[:, 0:1], CARRY[0:1, 0:P], ONE[0:1, 0:1], start=True, stop=True).then_inc(q["prep"], 1)
            pe.wait_ge(q["cnt_loaded"], 16)
            half = RC // 2
            tr(GATE[:, 0, 0:half], CNT_T[:, 0, :], ID[0:half, 0:half])
            tr(GATE[:, 0, P:P + half], CNT_T[:, 1, :], ID[0:half, 0:half]).then_inc(q["prep"], 1)
            pe.wait_ge(q["weights_ready"], 1)

            def rows_in(i, c):
                if c < SCALED // GC:
                    pe.wait_ge(q["xn_done"], i.times(1, 1))
                else:
                    pe.wait_ge(q["xn_scaled"], i.times(CHUNKS - SCALED // GC, c - SCALED // GC + 1))
                wait(pe, q["td_copied"], i.times(CHUNKS, c))
                for k in range(4):
                    g = GC * c + 2 * k
                    last = tr(TIN[:, P * k:P * k + P], XN[i.par][:, g:g + 2, :].rearrange("p g c -> p (g c)"), ID[:, :])
                last.then_inc(q["td_done"], 1)

            def gates(i, c, which=(0, 1, 2, 3)):
                pe.wait_ge(q["td_copied"], i.times(CHUNKS, c + 1))
                for g in which:
                    free = (q["sig_r"], q["sig_z"], q["t_u"], q["t_u"])[g]
                    wait(pe, free, i.times(CHUNKS, c))
                    mm(GATE[:, g, :], DW[:, g, :], HT[c % 2][:, :], start=True, stop=True).then_inc(q["gates_done"], 1)

            def rows_out(i, c):
                pe.wait_ge(q["y_ready"], i.times(CHUNKS, c + 1))
                wait(pe, q["out_done"], i.times(CHUNKS, c))
                for k in range(4):
                    last = tr(TOUT[:, P * k:P * k + P], Y[c % 2][:, P * k:P * k + P], ID[:, :])
                last.then_inc(q["to_done"], 1)

            def tiles_turned(of, done_, tiles=TILES):
                for t in range(tiles):
                    last = tr(EPT[:, t, :], of[:, t, :], ID[:, :])
                    if t % TH == TH - 1:
                        last.then_inc(done_, 1)

            def turn_moments(i):
                wait(pe, q["gru_u"], i.times(2))
                pe.wait_ge(q["std_ready"], i.times(1, 1))
                tiles_turned(MS, q["t2_done"])

            def turn_v(i):
                pe.wait_ge(q["norm_done"], i.times(1, 1))
                wait(pe, q["t2_copied"], i.times(2))
                tiles_turned(V, q["vt_done"])

            def messages(i, h):
                if h == 0:
                    pe.wait_ge(q["vt_copied"], i.times(2, 1))
                    pe.wait_ge(att_loaded[i.par], i.pair(16 * (PARTS + 1)))
                else:
                    wait(pe, q["od_done"], i.next(-1).times(2, 1))
                    pe.wait_ge(q["scan_done"], i.times(2, 1))
                cols = slice(HALF * h, HALF * h + HALF)
                att = ATT[i.par][:, cols]
                mm(EP[:, 0:HALF], QW[:, :], VTS[:, cols], start=True, stop=False)
                mm(EP[:, 0:HALF], WAUG[:, :], att, start=False, stop=True)
                if h == 0:
                    pe.wait_ge(q["vt_copied"], i.times(2, 2))
                mm(EP[:, HALF:EB], SELK[:, :], att, start=True, stop=True).then_inc(q["qk_done"], 1)

            def post(b, h, scans):
                pe.wait_ge(q["t2_copied"], b.times(2, 2))
                if scans is not None:
                    pe.wait_ge(q["scan_done"], scans.times(2, h + 1))
                for t in range(TH):
                    cols = slice(HALF * h + P * t, HALF * h + P * t + P)
                    mm(EPW[:, t, 0:3 * C], MST[:, cols], OW1[:, :], start=True, stop=False)
                    last = mm(EPW[:, t, 0:3 * C], MX[b.par][:, cols], OW2[:, :], start=False, stop=True)
                last.then_inc(q["o_done"], 1)

            def turn_sums(i):
                wait(pe, q["od_done"], i.times(2))
                pe.wait_ge(q["scan_done"], i.times(2, 2))
                for t in range(TILES):
                    last = tr(EPT[:, t, :], S[:, P * t:P * t + P], ID[:, :])
                last.then_inc(q["st_done"], 1)

            def turn_ho(b, sums):
                if sums is not None:
                    pe.wait_ge(q["ms_read"], sums.times(1, 1))
                pe.wait_ge(q["h_kept"], b.times(1, 1))
                pe.wait_ge(q["od_done"], b.times(2, 2 if sums is not None else 1))
                tiles_turned(HO[b.par], q["t3_done"], TILES if sums is not None else LAST_TILES)

            def edge_gates(b, h):
                if h:
                    pe.wait_ge(q["gru_u"], b.times(2, 1))
                for a in range(2):
                    if b.j is not None or b.off < BLOCKS - 1 or a == 0:
                        pe.wait_ge(q["t3_copied"], b.times(2, a + 1))
                    mm(EP[:, HALF * a:HALF * a + HALF], ONESB[:, :], SBIAS[:, :, :].rearrange("p a c -> p (a c)"),
                       start=True, stop=False, skip_group_check=True)
                    for t in (2 * a, 2 * a + 1):
                        cols = slice(HALF * h + P * t, HALF * h + P * t + P)
                        last = mm(EPW[:, t, :], HOT[:, cols], SW[:, :], start=False, stop=t % 2 == 1, skip_group_check=True)
                last.then_inc(q["g_done"], 1)

            def step(i, new=True, old=True):
                p, n = i.next(-1), i.next()
                rows_in(i, 1)
                messages(i, 0)
                gates(i, 1)
                if old:
                    post(p, 0, i)
                rows_out(i, 0)
                rows_in(i, 2)
                messages(i, 1)
                gates(i, 2)
                if old:
                    post(p, 1, i)
                rows_in(i, 3)
                rows_out(i, 1)
                turn_sums(i)
                gates(i, 3, (0, 1))
                if old:
                    turn_ho(p, i)
                    edge_gates(p, 0)
                gates(i, 3, (2,))
                gates(i, 3, (3,))
                if old:
                    edge_gates(p, 1)
                if new:
                    rows_in(n, 0)
                rows_out(i, 2)
                if new:
                    gates(n, 0, (0, 1))
                turn_moments(i)
                if new:
                    gates(n, 0, (2, 3))
                    turn_v(n)
                rows_out(i, 3)

            rows_in(At(None, 0), 0)
            gates(At(None, 0), 0)
            turn_v(At(None, 0))
            step(At(None, 0), old=False)
            step(At(None, 1))
            with pe.Fori(0, (BLOCKS - 3) // 2) as j:
                step(At(j, 2))
                step(At(j, 3))
            last = At(None, BLOCKS - 1)
            step(last, new=False)
            post(last, 0, None)
            turn_ho(last, None)
            edge_gates(last, 0)


def kernel(x, src, dst, edge_attr_4, L0_gnn_deg_hist, L0_gnn_weight, L0_gnn_W_e, L0_gnn_b_e, L0_gnn_W_pre, L0_gnn_b_pre,
           L0_gnn_W_post, L0_gnn_b_post, L0_gnn_W_ih, L0_gnn_W_hh, L0_gnn_b_ih, L0_gnn_b_hh):
    import numpy as np
    import concourse.bacc as bacc
    from concourse.bass_utils import run_bass_kernel_spmd

    x, src, dst, attr = (np.asarray(a) for a in (x, src, dst, edge_attr_4))
    pad = EDGES_PADDED - EDGES

    def padded(a, value):
        return np.concatenate([a, np.full((pad,) + a.shape[1:], value, a.dtype)])

    def by_tile(a):
        return a.reshape(ALL_TILES, P).T

    key = padded(dst, NODES)
    ends = np.full(1, NODES, dst.dtype), np.full(1, -1, dst.dtype)
    gidx = np.stack([by_tile(padded(dst, 0)), by_tile(padded(src, 0))], axis=2).reshape(P, 2 * ALL_TILES)
    attr = padded(attr, 0)
    w_ih, w_hh = np.asarray(L0_gnn_W_ih), np.asarray(L0_gnn_W_hh)
    b_ih, b_hh = np.asarray(L0_gnn_b_ih), np.asarray(L0_gnn_b_hh)
    w_t, w_pre, w_post = np.asarray(L0_gnn_weight)[0].T, np.asarray(L0_gnn_W_pre), np.asarray(L0_gnn_W_post)
    we_t = np.concatenate([np.asarray(L0_gnn_W_e), np.asarray(L0_gnn_b_e)[None]]).T

    def twice(a):
        return np.concatenate([a, a])

    aggregates = w_post[C:].reshape(3, 4, C, C)

    def stacked(upper, lower):
        return np.concatenate([np.concatenate(list(aggregates[:, a]), axis=1) for a in (upper, lower)])

    by_row = {"EW": by_tile(attr[:, 3]), "WIH2": twice(w_ih.T), "WHH2": twice(w_hh.T), "OW1": stacked(0, 3),
              "OW2": stacked(2, 1), "BIC": twice(b_ih.reshape(3, C).T), "BHC": twice(b_hh.reshape(3, C).T)}
    gates = w_ih.T.reshape(C, 3, 1, C)
    by_channel = {"WT2": np.concatenate([w_t, w_t], axis=1), "WPRE": np.concatenate(list(w_pre.reshape(3, C, C)), axis=1),
                  "WP0": w_post[0:C], "STDW": np.concatenate(list(aggregates[:, 3]), axis=1),
                  "WIHD": np.concatenate([gates, gates], axis=2).reshape(C, 6 * C), "WET": we_t,
                  "BPC": np.asarray(L0_gnn_b_post)[:, None]}
    along = key.reshape(P, RC), np.concatenate([ends[1], key[:-1]]).reshape(P, RC)
    arrays = {
        "x": x, "gidx": gidx,
        "keys": np.stack([by_tile(key), by_tile(np.concatenate([key[1:], ends[0]])), along[0], along[1]], axis=1),
        "key_b": key.reshape(BLOCKS, EB), "attr_r": attr.T.reshape(4, P, RC).transpose(1, 0, 2),
        "by_row": np.concatenate([by_row[n] for n in ROW_PARTS], axis=1),
        "by_channel": np.concatenate([by_channel[n] for n in CHANNEL_PARTS], axis=1),
        "biases": np.concatenate([b_ih, b_hh])[None], "b_pre": np.asarray(L0_gnn_b_pre)[None],
        "deg_hist": np.asarray(L0_gnn_deg_hist), "ident": np.eye(P, dtype=np.float32),
    }
    arrays = {k: np.ascontiguousarray(v) for k, v in arrays.items()}
    nc = bacc.Bacc("TRN2", target_bir_lowering=False, num_devices=1)
    args = {k: nc.dram_tensor("in_" + k, v.shape, mybir.dt.from_np(v.dtype), kind="ExternalInput").ap()
            for k, v in arrays.items()}
    out = nc.dram_tensor("out", (NODES, C), mybir.dt.float32, kind="ExternalOutput").ap()
    gnn_kernel(nc, out=out, **args)
    r = run_bass_kernel_spmd(nc, [{"in_" + k: v for k, v in arrays.items()}], core_ids=[0])
    return r.results[0]["out"]
```
